# Optimizing a Trainium2 kernel written in Bass

```python
import numpy as np
import jax
import jax.numpy as jnp

def _softmax(x, axis=-1):
    return jax.nn.softmax(x, axis=axis)

def _gelu(x):
    return jax.nn.gelu(x, approximate=True)

def _silu(x):
    return jax.nn.silu(x)

def _sigmoid(x):
    return jax.nn.sigmoid(x)

def _layernorm(x, axis=-1, eps=1e-05):
    m = jnp.mean(x, axis=axis, keepdims=True)
    v = jnp.var(x, axis=axis, keepdims=True)
    return (x - m) / jnp.sqrt(v + eps)

def _scatter_add(tgt, idx, src, axis=0):
    return tgt.at[idx].add(src)

def _segment_sum(src, seg, n):
    return jax.ops.segment_sum(src, seg, n)
kernel_name = 'mk_xattn_ffn_d1_seqx_r8_18908c'

def setup_inputs(seed: int=0):
    np.random.seed(seed)
    _w = jnp.asarray

    def _rec_inputs():
        import jax
        import jax.numpy as jnp
        _rk = jax.random.key(seed)
        x = -0.0002928 + 1 * jax.random.normal(jax.random.fold_in(_rk, 1), (32, 128, 128), jnp.float32)
        _lenS = 128 - jax.random.randint(jax.random.fold_in(_rk, 7), (32,), 0, max(1, 128 // 4) + 1, jnp.int32)
        _lenS2 = 77 - jax.random.randint(jax.random.fold_in(_rk, 8), (32,), 0, max(1, 77 // 4) + 1, jnp.int32)
        _ctx_1024P = jax.random.normal(jax.random.fold_in(_rk, 11), (32, 16, 128), jnp.float32)
        _ctx_1024c = jax.random.dirichlet(jax.random.fold_in(_rk, 511), 0.3 * jnp.ones((16,), jnp.float32), (32, 77))
        _ctx_1024t = jnp.einsum('bsk,bkd->bsd', _ctx_1024c, _ctx_1024P)
        _ctx_1024t = _ctx_1024t * jax.lax.rsqrt(jnp.mean(jnp.square(_ctx_1024t)) + 1e-12) * 0.953939
        ctx_1024 = -1.39393e-06 + 0.999914 * (_ctx_1024t + 0.3 * jax.random.normal(jax.random.fold_in(_rk, 611), (32, 77, 128), jnp.float32))
        _validS = jnp.arange(128)[None, :] < _lenS[:, None]
        _validS2 = jnp.arange(77)[None, :] < _lenS2[:, None]
        _causal = jnp.tril(jnp.ones((128, 128), dtype=bool))
        mask_1x1xSxS2_ik0 = jnp.where(jnp.broadcast_to(_validS2[0:1, None, None, :], (1, 1, 128, 77)), 0, 1).astype(jnp.int32)
        return (x, ctx_1024, mask_1x1xSxS2_ik0)
    x, ctx_1024, mask_1x1xSxS2_ik0 = _rec_inputs()

    def _L0_xattn_setup():
        import jax, jax.numpy as jnp
        import numpy as np
        import math
        D_MODEL = 128
        NUM_HEADS = 16
        B, S = (2, 256)
        key = jax.random.key(seed)
        ks = jax.random.split(key, 12)
        s = 0.02
        inp = {'q': jax.random.normal(ks[0], (B, S, D_MODEL), jnp.float32), 'k': jax.random.normal(ks[1], (B, S, D_MODEL), jnp.float32), 'v': jax.random.normal(ks[2], (B, S, D_MODEL), jnp.float32), 'W_q': jax.random.normal(ks[3], (D_MODEL, D_MODEL), jnp.float32) * s, 'b_q': jnp.zeros((D_MODEL,), jnp.float32), 'W_k': jax.random.normal(ks[4], (D_MODEL, D_MODEL), jnp.float32) * s, 'b_k': jnp.zeros((D_MODEL,), jnp.float32), 'W_v': jax.random.normal(ks[5], (D_MODEL, D_MODEL), jnp.float32) * s, 'b_v': jnp.zeros((D_MODEL,), jnp.float32), 'W_o': jax.random.normal(ks[6], (D_MODEL, D_MODEL), jnp.float32) * s, 'b_o': jnp.zeros((D_MODEL,), jnp.float32), 'mask': jnp.tril(jnp.ones((S, S), jnp.int32))[None, None, :, :]}
        return inp
    _L0_xattn_all = _L0_xattn_setup()
    _L0_xattn_in = {k: v for k, v in _L0_xattn_all.items() if k in ('W_q', 'b_q', 'W_k', 'b_k', 'W_v', 'b_v', 'W_o', 'b_o')}
    del _L0_xattn_all

    def _L0_ffn_setup():
        import jax, jax.numpy as jnp
        import numpy as np
        EPS = 1e-12

        def _l2norm(v):
            n = jnp.sqrt(jnp.sum(v * v, axis=-1, keepdims=True))
            return v / jnp.maximum(n, EPS)
        key = jax.random.key(seed)
        ks = jax.random.split(key, 6)
        B, S, D, F, E = (2, 256, 128, 512, 8)
        std = 0.02
        return {'x': jax.random.normal(ks[0], (B, S, D), jnp.float32), 'Wp': jax.random.normal(ks[1], (D, D), jnp.float32) * (1.0 / np.sqrt(D)), 'sim_matrix': jax.random.normal(ks[2], (E, D), jnp.float32) * std, 'temperature': jnp.asarray(1.0, jnp.float32), 'W1': jax.random.normal(ks[3], (E, D, F), jnp.float32) * (1.0 / np.sqrt(D)), 'b1': jnp.zeros((E, F), jnp.float32), 'W2': jax.random.normal(ks[4], (E, F, D), jnp.float32) * (1.0 / np.sqrt(F)), 'b2': jnp.zeros((E, D), jnp.float32)}
    _L0_ffn_all = _L0_ffn_setup()
    _L0_ffn_in = {k: v for k, v in _L0_ffn_all.items() if k in ('Wp', 'sim_matrix', 'temperature', 'W1', 'b1', 'W2', 'b2')}
    del _L0_ffn_all
    return {'x': x, 'ctx_1024': ctx_1024, 'mask_1x1xSxS2_ik0': mask_1x1xSxS2_ik0, 'L0_xattn_W_q': _L0_xattn_in['W_q'], 'L0_xattn_b_q': _L0_xattn_in['b_q'], 'L0_xattn_W_k': _L0_xattn_in['W_k'], 'L0_xattn_b_k': _L0_xattn_in['b_k'], 'L0_xattn_W_v': _L0_xattn_in['W_v'], 'L0_xattn_b_v': _L0_xattn_in['b_v'], 'L0_xattn_W_o': _L0_xattn_in['W_o'], 'L0_xattn_b_o': _L0_xattn_in['b_o'], 'L0_ffn_Wp': _L0_ffn_in['Wp'], 'L0_ffn_sim_matrix': _L0_ffn_in['sim_matrix'], 'L0_ffn_temperature': _L0_ffn_in['temperature'], 'L0_ffn_W1': _L0_ffn_in['W1'], 'L0_ffn_b1': _L0_ffn_in['b1'], 'L0_ffn_W2': _L0_ffn_in['W2'], 'L0_ffn_b2': _L0_ffn_in['b2']}

def reference(x, ctx_1024, mask_1x1xSxS2_ik0, L0_xattn_W_q, L0_xattn_b_q, L0_xattn_W_k, L0_xattn_b_k, L0_xattn_W_v, L0_xattn_b_v, L0_xattn_W_o, L0_xattn_b_o, L0_ffn_Wp, L0_ffn_sim_matrix, L0_ffn_temperature, L0_ffn_W1, L0_ffn_b1, L0_ffn_W2, L0_ffn_b2):
    import jax
    import jax.numpy as jnp

    def _L0_xattn_ref(q, k, v, W_q, b_q, W_k, b_k, W_v, b_v, W_o, b_o, mask):
        import jax, jax.numpy as jnp
        import numpy as np
        import math
        D_MODEL = 128
        NUM_HEADS = 16
        B, S = (2, 256)
        H, d_k = (NUM_HEADS, D_MODEL // NUM_HEADS)
        Bq, Sq, D = q.shape
        Sk = k.shape[1]
        qh = (q @ W_q.T + b_q).reshape(Bq, Sq, H, d_k).transpose(0, 2, 1, 3)
        kh = (k @ W_k.T + b_k).reshape(Bq, Sk, H, d_k).transpose(0, 2, 1, 3)
        vh = (v @ W_v.T + b_v).reshape(Bq, Sk, H, d_k).transpose(0, 2, 1, 3)
        scores = jnp.einsum('bhqd,bhkd->bhqk', qh, kh) / math.sqrt(d_k)
        scores = jnp.where(mask == 0, jnp.float32(-jnp.inf), scores)
        attn = jax.nn.softmax(scores, axis=-1)
        context = jnp.einsum('bhqk,bhkd->bhqd', attn, vh)
        context = context.transpose(0, 2, 1, 3).reshape(Bq, Sq, D)
        return context @ W_o.T + b_o

    def _L0_ffn_ref(x, Wp, sim_matrix, temperature, W1, b1, W2, b2):
        import jax, jax.numpy as jnp
        import numpy as np
        EPS = 1e-12

        def _l2norm(v):
            n = jnp.sqrt(jnp.sum(v * v, axis=-1, keepdims=True))
            return v / jnp.maximum(n, EPS)
        E = sim_matrix.shape[0]
        top_k = 2
        proj = jnp.einsum('bsd,ed->bse', x, Wp)
        pn = _l2norm(proj)
        sn = _l2norm(sim_matrix)
        gate_scores = jnp.einsum('bsd,ed->bse', pn, sn) / temperature
        top_v, top_i = jax.lax.top_k(gate_scores, top_k)
        gate_probs = jax.nn.softmax(top_v, axis=-1)
        comb = jnp.sum(jax.nn.one_hot(top_i, E, dtype=x.dtype) * gate_probs[..., None], axis=-2)
        h = jax.nn.gelu(jnp.einsum('bsd,edf->ebsf', x, W1) + b1[:, None, None, :], approximate=False)
        eo = jnp.einsum('ebsf,efd->ebsd', h, W2) + b2[:, None, None, :]
        out = jnp.einsum('ebsd,bse->bsd', eo, comb)
        return out
    x = x + _L0_xattn_ref(_layernorm(x, axis=-1), ctx_1024, ctx_1024, L0_xattn_W_q, L0_xattn_b_q, L0_xattn_W_k, L0_xattn_b_k, L0_xattn_W_v, L0_xattn_b_v, L0_xattn_W_o, L0_xattn_b_o, mask_1x1xSxS2_ik0)
    x = x + _L0_ffn_ref(_layernorm(x, axis=-1), L0_ffn_Wp, L0_ffn_sim_matrix, L0_ffn_temperature, L0_ffn_W1, L0_ffn_b1, L0_ffn_W2, L0_ffn_b2)
    return x

_drawn_inputs = setup_inputs


def setup_inputs(seed=0):
    import zlib

    import numpy as np

    out = dict(_drawn_inputs(seed))
    spreads = {'L0_xattn_b_q': (0.0, 0.8),
     'L0_xattn_b_k': (0.0, 0.8),
     'L0_xattn_b_v': (0.0, 0.1),
     'L0_xattn_b_o': (0.0, 0.1),
     'L0_ffn_b1': (0.0, 0.1),
     'L0_ffn_b2': (0.0, 0.1)}
    factors = {'L0_xattn_W_q': 4.285, 'L0_xattn_W_k': 6.181}
    for name, (base, spread) in spreads.items():
        noise = np.random.default_rng([zlib.crc32(name.encode()), seed]).standard_normal(out[name].shape)
        drawn = base * np.exp(spread * noise) if base else spread * noise
        out[name] = jnp.asarray(drawn.astype(out[name].dtype))
    for name, factor in factors.items():
        out[name] = (out[name] * factor).astype(out[name].dtype)
    return out
```

```python
import concourse.bass as bass
from concourse import mybir
from contextlib import ExitStack
import math


def xattn_moe_kernel(nc, x, ctx, mask, w_q, b_q, w_k, b_k, w_v, b_v, w_o, b_o,
                     w_p, sim, temp, w1, b1, w2, b2, out):
    f32, bf16, i32, u32 = mybir.dt.float32, mybir.dt.bfloat16, mybir.dt.int32, mybir.dt.uint32
    ALU, ACT, AX = mybir.AluOpType, mybir.ActivationFunctionType, mybir.AxisListType

    NB, S, D = x.shape
    SK = ctx.shape[1]
    NE, _, F = w1.shape
    H = 16
    DH = D // H
    P = 128
    assert S == P and D == P
    NTOK = NB * S
    TOPK = 2
    G = 4
    HG = H // G
    QR = P // G
    HB = 512 // SK
    SCALE = 1.0 / math.sqrt(DH)
    MASKED = -3.0e38
    LN_EPS = 1e-5
    NORM_EPS2 = 1e-24
    FC = F // P
    REGION = NTOK + P
    N_TILES = (NTOK * TOPK + NE * (P - 1)) // P
    SPARE = N_TILES - NTOK * TOPK // P
    ROW = 132
    SKIP = 1 << 20
    RING = 4
    FRING = 8
    N_CONSTS = 15
    TT = 72
    assert N_TILES <= TT

    lists = nc.dram_tensor("lists", (NE * REGION + SPARE * P, ROW), f32, kind="Internal").ap()
    results = nc.dram_tensor("results", (TOPK * NTOK, D), f32, kind="Internal").ap()

    est = ExitStack()
    with est:
        def sb(name, shape, dt=f32):
            return est.enter_context(nc.sbuf_tensor(name, shape, dt))

        def sem(name):
            return est.enter_context(nc.semaphore(name))

        identf = sb("identf", [P, P])
        identb = sb("identb", [P, P], bf16)
        tri = sb("tri", [P, P], bf16)
        onesb = sb("onesb", [P, P], bf16)
        headmask = sb("headmask", [P, H])
        neghalf = sb("neghalf", [P, 1])
        iota_e = sb("iota_e", [P, NE + 1])
        list_base = sb("list_base", [P, NE + 1])
        iota_t = sb("iota_t", [P, TT])
        dests = sb("dests", [P, NB, TOPK], i32)
        fill = sb("fill", [P, ROW])
        wnat = sb("wnat", [P, 5, P])
        wT = sb("wT", [P, 4, P])
        wqT, wkT, wvT, woT = (wT[:, n, :] for n in range(4))
        wg = sb("wg", [P, D + NE])
        simn = sb("simn", [NE, D])
        simd = sb("simd", [NE, D])
        simT = sb("simT", [P, NE])
        sim_sq = sb("sim_sq", [NE, D])
        sim_n2 = sb("sim_n2", [NE, 3])
        bq = sb("bq", [P, 1])
        bk = sb("bk", [P, 1])
        bo_row = sb("bo_row", [P, D])
        bo = sb("bo", [P, D])
        bv = sb("bv", [P, D])
        tempc = sb("tempc", [P, 1])
        invtemp = sb("invtemp", [P, 1])
        maski = sb("maski", [P, SK], i32)
        maskn = sb("maskn", [P, SK])
        anyk = sb("anyk", [P, 3])
        negb = sb("negb", [P, HB, SK], bf16)
        w1s = sb("w1s", [P, NE * F])
        w2s = sb("w2s", [P, NE * F])
        b1n = sb("b1n", [NE * FC, P])
        b1T = sb("b1T", [P, NE * FC])
        b2s = sb("b2s", [P, NE * D])
        xin = sb("xin", [P, RING, D])
        cin = sb("cin", [P, RING, D])
        st1 = sb("st1", [P, RING, 6])
        mv1 = sb("mv1", [P, RING, 2])
        ve1 = sb("ve1", [P, RING])
        rstd1 = sb("rstd1", [P, RING])
        xn = sb("xn", [P, 2, D])
        xT = sb("xT", [P, 2, P])
        qT = sb("qT", [P, 2, P])
        cT = sb("cT", [P, 2, SK])
        kT = sb("kT", [P, 2, SK])
        kbd = sb("kbd", [P, 2, H, SK])
        vpad = sb("vpad", [P, 2, G, HG * (QR + DH)])
        mx = sb("mx", [P, 2, H])
        pr = sb("pr", [P, 2, H, SK])
        sums = sb("sums", [P, 2, H])
        rec = sb("rec", [P, 2, H])
        recx = sb("recx", [P, 2, D])
        recT = sb("recT", [P, 2, P])
        pT = sb("pT", [P, G, HG * P])
        cxT = sb("cxT", [P, 2, P])
        x2 = sb("x2", [P, NB, D])
        st2 = sb("st2", [P, 2, 6])
        mv2 = sb("mv2", [P, 2, 2])
        ve2 = sb("ve2", [P, 2])
        rstd2 = sb("rstd2", [P, 2])
        rows = sb("rows", [P, RING, TOPK, ROW])
        xn2T = sb("xn2T", [P, 2, P])
        sq_junk = sb("sq_junk", [P, D])
        n2 = sb("n2", [P, 2])
        n2c = sb("n2c", [P, 2])
        rn = sb("rn", [P, 2])
        ginv = sb("ginv", [P, 2])
        dots = sb("dots", [P, 2, NE])
        gv = sb("gv", [P, NE])
        top8 = sb("top8", [P, 8])
        idx8 = sb("idx8", [P, 8], u32)
        diff = sb("diff", [P, NB])
        ohs = sb("ohs", [P, 2, TOPK, NE])
        sel = sb("sel", [P, 2, NE], bf16)
        selsum = sb("selsum", [P, 2, NE], bf16)
        rk = sb("rk", [P, NE])
        prod = sb("prod", [P, TOPK, NE])
        slots = sb("slots", [P, RING, TOPK], i32)
        cnt = sb("cnt", [P, NE])
        cnti = sb("cnti", [P, NE], i32)
        ntil_i = sb("ntil_i", [P, NE], i32)
        ntil = sb("ntil", [P, NE])
        ones8 = sb("ones8", [P, NE])
        cum = sb("cum", [P, NE])
        start9 = sb("start9", [P, NE + 1])
        cmp = sb("cmp", [P, TT, NE + 1])
        texp = sb("texp", [P, TT])
        rbase = sb("rbase", [P, TT])
        tab_w = sb("tab_w", [P, TT], i32)
        tab_c = sb("tab_c", [P, TT], i32)
        tab_b = sb("tab_b", [P, TT], i32)
        tab_r = sb("tab_r", [P, TT], i32)
        tmin = sb("tmin", [P, TT])
        fill_r = sb("fill_r", [P, NE], i32)
        expd = sb("expd", [P, NB])
        den = sb("den", [P, NB])
        p1 = sb("p1", [P, NB])
        p2 = sb("p2", [P, NB])
        xt = sb("xt", [P, FRING, ROW])
        w1c = sb("w1c", [P, 2, F])
        xtT = sb("xtT", [P, 2, P])
        h = sb("h", [P, 2, F])
        hT = sb("hT", [P, 2, F])
        eo = sb("eo", [P, FRING, D])
        CH = 8
        ys = sb("ys", [P, 2, TOPK, CH, D])

        ps_s = est.enter_context(nc.psum_tensor("ps_s", [P, 3, 512], f32))
        ps_t = est.enter_context(nc.psum_tensor("ps_t", [P, 2, 512], f32))
        ps_a = est.enter_context(nc.psum_tensor("ps_a", [P, 512], f32))
        ps_b = est.enter_context(nc.psum_tensor("ps_b", [P, 512], f32))
        ps_o = est.enter_context(nc.psum_tensor("ps_o", [P, 512], f32))

        l_w, l_c, l_w1, l_w2, l_b2 = (sem(n) for n in ("l_w", "l_c", "l_w1", "l_w2", "l_b2"))
        consts, filled, spare_filled = sem("consts"), sem("filled"), sem("spare_filled")
        wt_done, wt_copied, wpt_copied, simt_copied = (sem(n) for n in ("wt_done", "wt_copied", "wpt_copied", "simt_copied"))
        sim_sqd, sim_inv, sim_dir, simt_done, wgp_done, wgp_copied = (
            sem(n) for n in ("sim_sqd", "sim_inv", "sim_dir", "simt_done", "wgp_done", "wgp_copied"))
        mask_step, mask_ready, bo_ready = sem("mask_step"), sem("mask_ready"), sem("bo_ready")
        vzero, itemp = sem("vzero"), sem("itemp")
        x_loaded = [sem(f"x_loaded{r}") for r in range(RING)]
        c_loaded = [sem(f"c_loaded{r}") for r in range(RING)]
        scattered = [sem(f"scattered{r}") for r in range(RING)]
        names = ("bn1 ln1 var1 rs1 xn_ready xb_ready xT_done xT_ready q_done q_ready cT_done cT_ready k_done k_ready "
                 "kbd_ready v_done v_ready s01_done s2_done max01 max2 sub01 sub_done exp_done t0_done t1_done t2_done t3_done "
                 "t0_ready t1_ready t2_ready t3_ready sums_ready rec_ready recx_ready recT_done recT_ready av_done cx_ready "
                 "o_done x2_ready bn2 ln2 var2 rs2 xn2_ready dest_ready xn2T_done xn2T_ready g_done sq_ready dots_ready "
                 "n2_ready rn_ready ginv_ready gv_ready top_ready idx_ready diff_ready ohs_ready sel_ready selsum_ready "
                 "rank_done rk_ready prod_ready slot_ready").split()
        E = {n: sem(n) for n in names}
        cnt_done, tab_step, tab_ready, p_exp, p_step, exp_d = (
            sem(n) for n in ("cnt_done", "tab_step", "tab_ready", "p_exp", "p_step", "exp_d"))
        xt_loaded = [sem(f"xt_loaded{r}") for r in range(FRING)]
        returned = [sem(f"returned{r}") for r in range(FRING)]
        fnames = "xtT_done xtT_ready w1c_ready up_done h_ready act_ready down_done eo_ready".split()
        FE = {n: sem(n) for n in fnames}
        y_loaded = [sem(f"y_loaded{r}") for r in range(2)]
        sum1, sum2, stored = sem("sum1"), sem("sum2"), sem("stored")

        def known(b):
            return isinstance(b, int)

        def after(eng, s, b):
            assert known(b) or b.min_val >= 0
            if not known(b) or b >= 0:
                eng.wait_ge(s, b + 1)

        def settled(eng):
            eng.nop(nofuse=True)

        def after_dma(eng, ring, b, r, n=16):
            assert known(b) or b.min_val >= r
            if not known(b) or b >= 0:
                eng.wait_ge(ring[r], (b - r) * (n // len(ring)) + n)

        def steps(eng, step, first, last, lo, hi, body=RING):
            n = (hi - lo + 1) // body * body
            for i in range(first, lo):
                step(i, i)
            with eng.Fori(lo, lo + n - body + 1, body) as i0:
                for u in range(body):
                    step(i0 + u, lo + u)
            for i in range(lo + n, last + 1):
                step(i, i)

        def has(i, k, n=NB):
            return not known(i) or 0 <= i + k < n

        def at(ap, b):
            return ap[:, b, :] if known(b) else ap[:, bass.ds(b, 1), :].rearrange("p a n -> p (a n)")

        block = est.enter_context(nc.Block())

        @block.sync
        def _(sp):
            def step(i, m):
                b, r = i, m % RING
                if has(i, 0):
                    after(sp, E["xn_ready"], b - RING)
                    after(sp, E["xb_ready"], b - RING)
                    sp.dma_start(xin[:, r, :], x[b, :, :] if known(b) else x[bass.ds(b, 1), :, :].rearrange("a s d -> (a s) d")
                                 ).then_inc(x_loaded[r], 16)
                    after(sp, E["cT_done"], b - RING)
                    sp.dma_start(cin[0:SK, r, :], ctx[b, :, :] if known(b) else ctx[bass.ds(b, 1), :, :].rearrange("a s d -> (a s) d")
                                 ).then_inc(c_loaded[r], 16)

            steps(sp, step, 0, NB - 1, RING, NB - 1)

            sp.wait_ge(filled, 1)
            for n in range(SPARE):
                sp.dma_start(lists[NE * REGION + n * P:NE * REGION + (n + 1) * P, :], fill[:, :]).then_inc(spare_filled, 16)
            sp.wait_ge(tab_ready, 1)
            for e in range(NE):
                row = sp.value_load(fill_r[0:1, e:e + 1], min_val=e * REGION, max_val=e * REGION + NTOK)
                sp.dma_start(lists[bass.ds(row, P), :], fill[:, :]).then_inc(spare_filled, 16)
            sp.wait_ge(spare_filled, 16 * (SPARE + NE))
            for r in range(RING):
                sp.wait_ge(scattered[r], NB // RING * 16 * TOPK)

            def load_tile(j, m):
                r = m % FRING
                after(sp, FE["xtT_done"], j - FRING)
                after_dma(sp, returned, j - FRING, r)
                row = sp.value_load(tab_r[0:1, j:j + 1] if known(j) else tab_r[0:1, bass.ds(j, 1)],
                                    min_val=0, max_val=NE * REGION + (SPARE - 1) * P)
                sp.dma_start(xt[:, r, :], lists[bass.ds(row, P), :]).then_inc(xt_loaded[r], 16)

            steps(sp, load_tile, 0, N_TILES - 1, FRING, N_TILES - 1, FRING)

            for r in range(FRING):
                sp.wait_ge(returned[r], len(range(r, N_TILES, FRING)) * 16)
            res = results.rearrange("(k c t p) d -> c k p t d", k=TOPK, t=CH, p=P)
            for c in range(NB // CH):
                if c >= 2:
                    sp.wait_ge(sum2, CH * (c - 1))
                for k in range(TOPK):
                    sp.dma_start(ys[:, c % 2, k, :, :], res[c, k]).then_inc(y_loaded[c % 2], 16)
            for c in range(NB // CH):
                sp.wait_ge(sum2, CH * (c + 1))
                sp.dma_start(out[c * CH:(c + 1) * CH, :, :].rearrange("t p d -> p t d"), x2[:, c * CH:(c + 1) * CH, :]
                             ).then_inc(stored, 16)
            sp.wait_ge(stored, 16 * (NB // CH))

        @block.gpsimd
        def _(pool):
            nc.gpsimd.memset(identf[:, :], 0.0).then_inc(consts, 1)
            nc.gpsimd.memset(onesb[:, :], 1.0).then_inc(consts, 1)
            nc.gpsimd.memset(headmask[:, :], 1.0).then_inc(consts, 1)
            nc.gpsimd.memset(neghalf[:, :], -0.5).then_inc(consts, 1)
            nc.gpsimd.memset(fill[:, :], 0.0).then_inc(consts, 1)
            nc.gpsimd.memset(selsum[:, 0, :], 0.0).then_inc(consts, 1)
            pool.wait_ge(consts, 6)
            nc.gpsimd.affine_select(out=identf[:, :], in_=identf[:, :], compare_op=ALU.not_equal, fill=1.0, base=0,
                                    pattern=[[-1, P]], channel_multiplier=1).then_inc(consts, 1)
            nc.gpsimd.affine_select(out=tri[:, :], in_=onesb[:, :], compare_op=ALU.is_gt, fill=0.0, base=0,
                                    pattern=[[1, P]], channel_multiplier=-1).then_inc(consts, 1)
            nc.gpsimd.affine_select(out=headmask[:, :], in_=headmask[:, :], compare_op=ALU.is_ge, fill=0.0, base=0,
                                    pattern=[[-DH, H]], channel_multiplier=1).then_inc(consts, 1)
            pool.wait_ge(consts, 9)
            nc.gpsimd.affine_select(out=headmask[:, :], in_=headmask[:, :], compare_op=ALU.is_ge, fill=0.0, base=DH - 1,
                                    pattern=[[DH, H]], channel_multiplier=-1).then_inc(consts, 1)
            nc.gpsimd.tensor_copy(identb[:, :], identf[:, :]).then_inc(consts, 1)
            nc.gpsimd.iota(iota_e[:, :], [[1, NE + 1]], base=0, channel_multiplier=0,
                           allow_small_or_imprecise_dtypes=True).then_inc(consts, 1)
            nc.gpsimd.iota(list_base[:, :], [[REGION, NE + 1]], base=0, channel_multiplier=0,
                           allow_small_or_imprecise_dtypes=True).then_inc(consts, 1)
            nc.gpsimd.iota(iota_t[:, :], [[1, TT]], base=0, channel_multiplier=0,
                           allow_small_or_imprecise_dtypes=True).then_inc(consts, 1)
            nc.gpsimd.iota(dests[:, :, :], [[P, NB], [NTOK, TOPK]], base=0, channel_multiplier=1).then_inc(consts, 1)
            nc.gpsimd.iota(fill[:, D:D + 1].bitcast(i32), [[1, 1]], base=SKIP, channel_multiplier=0).then_inc(filled, 1)
            pool.wait_ge(consts, N_CONSTS)

            pool.wait_ge(sim_sqd, 1)
            nc.gpsimd.tensor_scalar(sim_n2[:, 1:2], sim_n2[:, 0:1], NORM_EPS2, 1.0, ALU.max, ALU.mult).then_inc(sim_inv, 1)
            pool.wait_ge(sim_inv, 1)
            nc.gpsimd.tensor_tensor(sim_n2[:, 2:3], sim_n2[:, 1:2], neghalf[0:NE, :], ALU.pow).then_inc(sim_inv, 1)
            pool.wait_ge(vzero, 3)
            pool.wait_ge(bo_ready, 1)
            pool.wait_ge(itemp, 1)

            def step(i, m):
                if has(i, -4):
                    b, r = i - 4, (m - 4) % 2
                    after(pool, E["sq_ready"], b)
                    settled(pool)
                    nc.gpsimd.tensor_scalar(n2c[:, r:r + 1], n2[:, r:r + 1], NORM_EPS2, 1.0, ALU.max, ALU.mult
                                            ).then_inc(E["n2_ready"], 1)
                    after(pool, E["n2_ready"], b)
                    nc.gpsimd.tensor_tensor(rn[:, r:r + 1], n2c[:, r:r + 1], neghalf[:, :], ALU.pow).then_inc(E["rn_ready"], 1)
                    after(pool, E["rn_ready"], b)
                    after(pool, E["gv_ready"], b - 2)
                    nc.gpsimd.tensor_tensor(ginv[:, r:r + 1], rn[:, r:r + 1], invtemp[:, :], ALU.mult
                                            ).then_inc(E["ginv_ready"], 1)
                if has(i, 2):
                    b, r = i + 2, (m + 2) % RING
                    after(pool, E["ln1"], b)
                    settled(pool)
                    nc.gpsimd.tensor_scalar(ve1[:, r:r + 1], mv1[:, r, 1:2], LN_EPS, 1.0, ALU.add, ALU.mult).then_inc(E["var1"], 1)
                    after(pool, E["var1"], b)
                    after(pool, E["xn_ready"], b - RING)
                    nc.gpsimd.tensor_tensor(rstd1[:, r:r + 1], ve1[:, r:r + 1], neghalf[:, :], ALU.pow).then_inc(E["rs1"], 1)
                if has(i, 1):
                    b, r = i + 1, (m + 1) % RING
                    after_dma(pool, x_loaded, b, r)
                    nc.gpsimd.tensor_tensor(at(x2, b), xin[:, r, :], bo[:, :], ALU.add).then_inc(E["xb_ready"], 1)
                if has(i, -6):
                    b, r = i - 6, (m - 6) % RING
                    after(pool, E["slot_ready"], b)
                    after(pool, E["dest_ready"], b)
                    after(pool, E["xn2_ready"], b)
                    settled(pool)
                    for k in range(TOPK):
                        nc.gpsimd.indirect_dma_start(lists, bass.IndirectOffsetOnAxis(ap=slots[:, r, k:k + 1], axis=0),
                                                     rows[:, r, k, :], None).then_inc(scattered[r], 16)
                if has(i, -2):
                    b, r = i - 2, (m - 2) % RING
                    after_dma(pool, scattered, b - RING, r, 16 * TOPK)
                    settled(pool)
                    d = dests[:, b, :] if known(b) else dests[:, bass.ds(b, 1), :].rearrange("p a n -> p (a n)")
                    nc.gpsimd.tensor_copy(rows[:, r, :, D:D + 1].rearrange("p k o -> p (k o)").bitcast(i32), d
                                          ).then_inc(E["dest_ready"], 1)
                    r = (m - 2) % 2
                    after(pool, E["ln2"], b)
                    settled(pool)
                    nc.gpsimd.tensor_scalar(ve2[:, r:r + 1], mv2[:, r, 1:2], LN_EPS, 1.0, ALU.add, ALU.mult).then_inc(E["var2"], 1)
                    after(pool, E["var2"], b)
                    after(pool, E["xn2_ready"], b - 2)
                    nc.gpsimd.tensor_tensor(rstd2[:, r:r + 1], ve2[:, r:r + 1], neghalf[:, :], ALU.pow).then_inc(E["rs2"], 1)
                if has(i, 2):
                    b, r = i + 2, (m + 2) % 2
                    after(pool, E["k_ready"], b)
                    after(pool, E["s2_done"], b - 2)
                    nc.gpsimd.tensor_tensor(kbd[:, r, :, :], kT[:, r, :].unsqueeze(1).to_broadcast([P, H, SK]),
                                            headmask[:, :].unsqueeze(2).to_broadcast([P, H, SK]), ALU.mult
                                            ).then_inc(E["kbd_ready"], 1)

            steps(pool, step, -2, NB + 5, 6, NB - 3)

            def give_back(j, m):
                r = m % FRING
                after(pool, FE["eo_ready"], j)
                settled(pool)
                nc.gpsimd.indirect_dma_start(results, bass.IndirectOffsetOnAxis(ap=xt[:, r, D:D + 1].bitcast(i32), axis=0),
                                             eo[:, r, :], None, bounds_check=TOPK * NTOK - 1, oob_is_err=False
                                             ).then_inc(returned[r], 16)

            steps(pool, give_back, 0, N_TILES - 1, 0, N_TILES - 1, FRING)

        @block.tensor
        def _(pe):
            pe.wait_ge(l_w, 16 * 7)
            pe.wait_ge(consts, N_CONSTS)
            for n in range(4):
                last = nc.tensor.transpose(ps_t[:, 0, n * P:(n + 1) * P], wnat[:, n, :], identf[:, :])
            last.then_inc(wt_done, 1)
            nc.tensor.transpose(ps_t[:, 1, 0:P], wnat[:, 4, :], identf[:, :])
            nc.tensor.transpose(ps_t[:, 1, P:P + NE * FC], b1n[:, :], identf[0:NE * FC, 0:NE * FC]).then_inc(wt_done, 1)
            pe.wait_ge(sim_dir, 1)
            nc.tensor.transpose(ps_a[:, 0:NE], simd[:, :], identf[0:NE, 0:NE]).then_inc(simt_done, 1)
            pe.wait_ge(simt_copied, 1)
            nc.tensor.matmul(ps_b[:, 0:NE], wnat[:, 4, :], simT[:, :], start=True, stop=True).then_inc(wgp_done, 1)
            pe.wait_ge(wt_copied, 1)
            pe.wait_ge(wpt_copied, 2)
            pe.wait_ge(wgp_copied, 1)
            pe.wait_ge(mask_ready, 1)

            def scores(r, bank, h0, nh):
                n = nh * SK
                keys = kbd[:, r, h0:h0 + nh, :].rearrange("p h k -> p (h k)")
                nc.tensor.matmul(ps_s[:, bank, 0:n], qT[:, r, :], keys, start=True, stop=False)
                return nc.tensor.matmul(ps_s[:, bank, 0:n], identb[:, :],
                                        negb[:, 0:nh, :].rearrange("p h k -> p (h k)"), start=False, stop=True)

            def probs_T(b, m, g):
                r = m % 2
                for j in range(HG):
                    last = nc.tensor.transpose(ps_t[0:SK, g % 2, j * P:(j + 1) * P], pr[:, r, g * HG + j, :], identf[:, :])
                last.then_inc(E[f"t{g}_done"], 1)

            def step(i, m):
                r0, r1 = m % 2, (m + 1) % 2
                if has(i, 0):
                    after(pe, E["q_ready"], i)
                    after(pe, E["kbd_ready"], i)
                    after(pe, E["sub_done"], i - 1)
                    scores(r0, 0, 0, HB)
                if has(i, -2):
                    after(pe, E["cx_ready"], i - 2)
                    after(pe, E["xn2T_ready"], i - 4)
                    if not has(i, -4):
                        after(pe, E["recT_ready"], i - 2)
                    nc.tensor.matmul(ps_a[:, 0:D], cxT[:, r0, :], woT, start=True, stop=True).then_inc(E["o_done"], 1)
                if has(i, 0):
                    scores(r0, 1, HB, HB).then_inc(E["s01_done"], 1)
                    after(pe, E["cT_ready"], i)
                    after(pe, E["dots_ready"], i - 4)
                    after(pe, E["sq_ready"], i - 4)
                    if not has(i, -4):
                        after(pe, E["k_ready"], i + 1)
                    nc.tensor.matmul(ps_b[0:SK, 0:D], cT[:, r0, :], wvT, start=True, stop=True).then_inc(E["v_done"], 1)
                    scores(r0, 2, 2 * HB, H - 2 * HB).then_inc(E["s2_done"], 1)
                if has(i, -1):
                    after(pe, E["exp_done"], i - 1)
                    after(pe, E["t2_ready"], i - 2)
                    probs_T(i - 1, r1, 0)
                    after(pe, E["t3_ready"], i - 2)
                    probs_T(i - 1, r1, 1)
                if has(i, 2):
                    after_dma(pe, c_loaded, i + 2, (m + 2) % RING)
                    after(pe, E["v_ready"], i if not known(i) else min(i, NB - 1))
                    if not has(i, 0):
                        after(pe, E["k_ready"], i + 1)
                    nc.tensor.transpose(ps_b[:, 0:SK], cin[0:SK, (m + 2) % RING, :], identf[0:SK, 0:SK]).then_inc(E["cT_done"], 1)
                if has(i, 1):
                    after(pe, E["xn_ready"], i + 1)
                    after(pe, E["x2_ready"], i - 2)
                    if not has(i, -2):
                        after(pe, E["q_ready"], i)
                    nc.tensor.transpose(ps_a[:, 0:P], xn[:, r1, :], identf[:, :]).then_inc(E["xT_done"], 1)
                if has(i, -1):
                    after(pe, E["t0_ready"], i - 1)
                    probs_T(i - 1, r1, 2)
                    after(pe, E["t1_ready"], i - 1)
                    probs_T(i - 1, r1, 3)
                if has(i, 2):
                    after(pe, E["cT_ready"], i + 2)
                    nc.tensor.matmul(ps_b[:, 0:SK], wkT, cT[:, r0, :], start=True, stop=True).then_inc(E["k_done"], 1)
                if has(i, 1):
                    after(pe, E["xT_ready"], i + 1)
                    nc.tensor.matmul(ps_a[:, 0:P], wqT, xT[:, r1, :], start=True, stop=True).then_inc(E["q_done"], 1)
                if has(i, -1):
                    after(pe, E["recx_ready"], i - 1)
                    if has(i, 1):
                        after(pe, E["q_ready"], i + 1)
                    elif has(i, -2):
                        after(pe, E["x2_ready"], i - 2)
                    nc.tensor.transpose(ps_a[:, 0:P], recx[:, r1, :], identf[:, :]).then_inc(E["recT_done"], 1)
                if has(i, -5):
                    after(pe, E["sel_ready"], i - 5)
                    after(pe, E["selsum_ready"], i - 6)
                    if has(i, 2):
                        after(pe, E["k_ready"], i + 2)
                    else:
                        after(pe, E["v_ready"], min(i, NB - 1))
                        after(pe, E["dots_ready"], i - 4 if i - 4 < NB else NB - 1)
                        after(pe, E["sq_ready"], i - 4 if i - 4 < NB else NB - 1)
                    nc.tensor.matmul(ps_b[:, 256:256 + NE], tri[:, :], sel[:, r1, :], start=True, stop=False)
                    nc.tensor.matmul(ps_b[:, 256:256 + NE], onesb[:, :], selsum[:, r1, :], start=False, stop=True
                                     ).then_inc(E["rank_done"], 1)
                if has(i, -3):
                    after(pe, E["xn2_ready"], i - 3)
                    if has(i, -1):
                        after(pe, E["recT_ready"], i - 1)
                    elif has(i, -2):
                        after(pe, E["x2_ready"], i - 2)
                    nc.tensor.transpose(ps_a[:, 0:P], rows[:, (m - 3) % RING, 0, 0:D], identf[:, :]).then_inc(E["xn2T_done"], 1)
                if has(i, -1):
                    after(pe, E["t2_ready"], i - 1)
                    after(pe, E["t3_ready"], i - 1)
                    after(pe, E["v_ready"], i - 1)
                    after(pe, E["cx_ready"], i - 2)
                    for j in range(HG):
                        for g in range(G):
                            last = nc.tensor.matmul(ps_o[g * QR:(g + 1) * QR, 0:P], vpad[0:SK, r1, g, j * QR:(j + 1) * QR],
                                                    pT[0:SK, g, j * P:(j + 1) * P], start=(j == 0), stop=(j == HG - 1),
                                                    tile_position=(0, g * QR))
                    last.then_inc(E["av_done"], 1)
                if has(i, -3):
                    after(pe, E["xn2T_ready"], i - 3)
                    after(pe, E["rk_ready"], i - 5)
                    if not has(i, -5):
                        after(pe, E["k_ready"], i + 2 if has(i, 2) else -1)
                    nc.tensor.matmul(ps_b[:, 0:D + NE], xn2T[:, r1, :], wg[:, :], start=True, stop=True).then_inc(E["g_done"], 1)

            steps(pe, step, -2, NB + 4, 6, NB - 3)

            after(pe, E["selsum_ready"], NB - 1)
            after(pe, E["rk_ready"], NB - 1)
            nc.tensor.matmul(ps_b[:, 0:NE], onesb[:, :], selsum[:, NB % 2, :], start=True, stop=True).then_inc(cnt_done, 1)

            pe.wait_ge(l_w2, 16)
            pe.wait_ge(tab_ready, 1)
            ps_x = [ps_a, ps_b]
            ps_e = [ps_o, ps_s[:, 2, :]]

            def tile(j, m):
                if has(j, 2, N_TILES):
                    r, q = m % 2, (m + 2) % FRING
                    after_dma(pe, xt_loaded, j + 2, q)
                    after(pe, FE["xtT_ready"], j)
                    nc.tensor.transpose(ps_x[r][:, 0:P], xt[:, q, 0:D], identf[:, :]).then_inc(FE["xtT_done"], 1)
                if has(j, 1, N_TILES):
                    r = (m + 1) % 2
                    after(pe, FE["xtT_ready"], j + 1)
                    after(pe, FE["w1c_ready"], j + 1)
                    after(pe, FE["h_ready"], j - 1)
                    for c in range(FC):
                        last = nc.tensor.matmul(ps_s[:, r, c * P:(c + 1) * P], w1c[:, r, c * P:(c + 1) * P], xtT[:, r, :],
                                                start=True, stop=True)
                    last.then_inc(FE["up_done"], 1)
                if has(j, -1, N_TILES):
                    r = (m - 1) % 2
                    b = j - 1
                    e = pe.value_load(tab_w[0:1, b:b + 1] if known(b) else tab_w[0:1, bass.ds(b, 1)],
                                      min_val=0, max_val=(NE - 1) * F)
                    after(pe, FE["act_ready"], j - 1)
                    after(pe, FE["eo_ready"], j - 3)
                    for c in range(FC):
                        last = nc.tensor.matmul(ps_e[r][:, 0:D], hT[:, r, c * P:(c + 1) * P], w2s[:, bass.ds(e + c * D, D)],
                                                start=(c == 0), stop=(c == FC - 1))
                    last.then_inc(FE["down_done"], 1)

            steps(pe, tile, -2, N_TILES, 3, N_TILES - 3, FRING)

        @block.scalar
        def _(act):
            for n, w in enumerate((w_q, w_k, w_v, w_o, w_p)):
                act.dma_start(wnat[:, n, :], w).then_inc(l_w, 16)
            act.dma_start(simn[:, :], sim).then_inc(l_w, 16)
            act.dma_start(b1n[:, :], b1.rearrange("e (c f) -> (e c) f", f=P)).then_inc(l_w, 16)
            act.dma_start(bq[:, :], b_q.rearrange("(p o) -> p o", o=1)).then_inc(l_c, 16)
            act.dma_start(bk[:, :], b_k.rearrange("(p o) -> p o", o=1)).then_inc(l_c, 16)
            act.dma_start(maski[:, :], mask.rearrange("a b q k -> (a b q) k")).then_inc(l_c, 16)
            act.dma_start(bo_row[:, :], b_o.partition_broadcast(P)).then_inc(l_c, 16)
            act.dma_start(bv[:, :], b_v.partition_broadcast(P)).then_inc(l_c, 16)
            act.dma_start(tempc[:, :], temp.partition_broadcast(P)).then_inc(l_c, 16)
            act.dma_start(w1s[:, :].rearrange("p (e f) -> p e f", e=NE), w1.rearrange("e d f -> d e f")).then_inc(l_w1, 16)
            act.dma_start(w2s[:, :].rearrange("p (e c d) -> p e c d", e=NE, c=FC),
                          w2.rearrange("e (c p) d -> p e c d", p=P)).then_inc(l_w2, 16)
            act.dma_start(b2s[:, :], b2.rearrange("e d -> (e d)").partition_broadcast(P)).then_inc(l_b2, 16)
            act.wait_ge(l_w, 16 * 7)
            nc.scalar.activation(sim_sq[:, :], simn[:, :], ACT.Square, accum_out=sim_n2[:, 0:1]).then_inc(sim_sqd, 1)
            act.wait_ge(sim_inv, 2)
            nc.scalar.activation(simd[:, :], simn[:, :], ACT.Copy, scale=sim_n2[:, 2:3]).then_inc(sim_dir, 1)
            act.wait_ge(wt_done, 1)
            nc.scalar.activation(wT[:, :, :].rearrange("p n m -> p (n m)"), ps_t[:, 0, :], ACT.Copy).then_inc(wt_copied, 1)
            act.wait_ge(wt_done, 2)
            nc.scalar.activation(wg[:, 0:D], ps_t[:, 1, 0:P], ACT.Copy).then_inc(wpt_copied, 1)
            nc.scalar.activation(b1T[:, :], ps_t[:, 1, P:P + NE * FC], ACT.Copy).then_inc(wpt_copied, 1)
            act.wait_ge(simt_done, 1)
            nc.scalar.activation(simT[:, :], ps_a[:, 0:NE], ACT.Copy).then_inc(simt_copied, 1)
            act.wait_ge(wgp_done, 1)
            nc.scalar.activation(wg[:, D:D + NE], ps_b[:, 0:NE], ACT.Copy).then_inc(wgp_copied, 1)
            act.wait_ge(l_c, 16 * 6)

            def probs_out(i, g):
                after(act, E[f"t{g}_done"], i - 1)
                after(act, E["av_done"], i - 2)
                nc.scalar.activation(pT[0:SK, g, :], ps_t[0:SK, g % 2, :], ACT.Copy).then_inc(E[f"t{g}_ready"], 1)

            def step(i, m):
                r0, r1 = m % 2, (m + 1) % 2
                if has(i, -1):
                    probs_out(i, 0)
                    probs_out(i, 1)
                if has(i, 2):
                    after(act, E["cT_done"], i + 2)
                    after(act, E["v_done"], i)
                    after(act, E["k_done"], i)
                    nc.scalar.activation(cT[:, r0, :], ps_b[:, 0:SK], ACT.Copy).then_inc(E["cT_ready"], 1)
                if has(i, 1):
                    after(act, E["xT_done"], i + 1)
                    after(act, E["q_done"], i - 1)
                    nc.scalar.activation(xT[:, r1, :], ps_a[:, 0:P], ACT.Copy).then_inc(E["xT_ready"], 1)
                if has(i, -1):
                    probs_out(i, 2)
                    probs_out(i, 3)
                if has(i, 2):
                    after(act, E["k_done"], i + 2)
                    after(act, E["kbd_ready"], i)
                    nc.scalar.activation(kT[:, r0, :], ps_b[:, 0:SK], ACT.Identity, bias=bk[:, 0:1]).then_inc(E["k_ready"], 1)
                if has(i, 1):
                    after(act, E["q_done"], i + 1)
                    after(act, E["s2_done"], i - 1)
                    nc.scalar.activation(qT[:, r1, :], ps_a[:, 0:P], ACT.Identity, bias=bq[:, 0:1]).then_inc(E["q_ready"], 1)
                if has(i, -1):
                    after(act, E["recT_done"], i - 1)
                    after(act, E["cx_ready"], i - 3)
                    nc.scalar.activation(recT[:, r1, :], ps_a[:, 0:P], ACT.Copy).then_inc(E["recT_ready"], 1)
                if has(i, -3):
                    after(act, E["xn2T_done"], i - 3)
                    after(act, E["g_done"], i - 5)
                    nc.scalar.activation(xn2T[:, r1, :], ps_a[:, 0:P], ACT.Copy).then_inc(E["xn2T_ready"], 1)
                if has(i, 0):
                    after(act, E["sub_done"], i)
                    p = pr[:, r0, :, :].rearrange("p h k -> p (h k)")
                    nc.scalar.activation(p, p, ACT.Exp, scale=SCALE).then_inc(E["exp_done"], 1)
                if has(i, -3):
                    after(act, E["g_done"], i - 3)
                    after(act, E["ginv_ready"], i - 5)
                    if not known(i) or i - 4 >= 0:
                        after(act, E["sq_ready"], i - 4)
                    nc.scalar.activation(sq_junk[:, :], ps_b[:, 0:D], ACT.Square, accum_out=n2[:, r1:r1 + 1]
                                         ).then_inc(E["sq_ready"], 1)
                    after(act, E["gv_ready"], i - 5)
                    nc.scalar.activation(dots[:, r1, :], ps_b[:, D:D + NE], ACT.Copy).then_inc(E["dots_ready"], 1)

            steps(act, step, -2, NB + 2, 5, NB - 3)

            act.wait_ge(p_step, 0 + 1)
            nc.scalar.activation(expd[:, :], diff[:, :], ACT.Exp).then_inc(p_exp, 1)

            act.wait_ge(l_w1, 16)
            act.wait_ge(tab_ready, 1)

            def tile(j, m):
                r = m % 2
                if has(j, 2, N_TILES):
                    b = j + 2
                    e = act.value_load(tab_w[0:1, b:b + 1] if known(b) else tab_w[0:1, bass.ds(b, 1)],
                                       min_val=0, max_val=(NE - 1) * F)
                    after(act, FE["up_done"], j)
                    settled(act)
                    nc.scalar.activation(w1c[:, r, :], w1s[:, bass.ds(e, F)], ACT.Copy).then_inc(FE["w1c_ready"], 1)
                if has(j, 0, N_TILES):
                    after(act, FE["h_ready"], j)
                    after(act, FE["down_done"], j - 2)
                    nc.scalar.activation(hT[:, r, :], h[:, r, :], ACT.Gelu).then_inc(FE["act_ready"], 1)

            steps(act, tile, -2, N_TILES - 1, 2, N_TILES - 3, FRING)

        @block.vector
        def _(dve):
            nc.vector.memset(vpad[:, :, :, :], 0.0).then_inc(vzero, 1)
            nc.vector.memset(ones8[:, :], 1.0).then_inc(vzero, 1)
            nc.vector.memset(rows[:, :, :, :], 0.0).then_inc(vzero, 1)
            dve.wait_ge(vzero, 3)
            dve.wait_ge(l_c, 16 * 6)
            dve.wait_ge(consts, N_CONSTS)
            nc.vector.reciprocal(invtemp[:, :], tempc[:, :]).then_inc(itemp, 1)
            nc.vector.tensor_scalar(negb[:, :, :], maski[:, :].unsqueeze(1).to_broadcast([P, HB, SK]), 0.0, MASKED,
                                    ALU.is_equal, ALU.mult).then_inc(mask_ready, 1)
            nc.vector.tensor_scalar(maskn[:, :], maski[:, :], 0.0, None, ALU.not_equal).then_inc(mask_step, 1)
            dve.wait_ge(mask_step, 1)
            nc.vector.tensor_reduce(anyk[:, 0:1], maskn[:, :], AX.X, ALU.max).then_inc(mask_step, 1)
            dve.wait_ge(mask_step, 2)
            nc.vector.reciprocal(anyk[:, 1:2], anyk[:, 0:1]).then_inc(mask_step, 1)
            dve.wait_ge(mask_step, 3)
            nc.vector.tensor_scalar(anyk[:, 2:3], anyk[:, 1:2], 0.0, None, ALU.mult).then_inc(mask_step, 1)
            dve.wait_ge(mask_step, 4)
            nc.vector.tensor_scalar(bo[:, :], bo_row[:, :], anyk[:, 2:3], None, ALU.add).then_inc(bo_ready, 1)

            def bank(bk0, nb, nh):
                return ps_s[:, bk0:bk0 + nb, 0:nh * SK].rearrange("p n (h k) -> p n h k", k=SK)

            def step(i, m):
                r0, r1 = m % 2, (m + 1) % 2
                if has(i, -1):
                    after(dve, E["exp_done"], i - 1)
                    nc.vector.tensor_reduce(sums[:, r1, :], pr[:, r1, :, :], AX.X, ALU.add).then_inc(E["sums_ready"], 1)
                    after(dve, E["sums_ready"], i - 1)
                    nc.vector.reciprocal(rec[:, r1, :], sums[:, r1, :]).then_inc(E["rec_ready"], 1)
                    after(dve, E["rec_ready"], i - 1)
                    after(dve, E["recT_done"], i - 3)
                    nc.vector.tensor_copy(recx[:, r1, :].rearrange("p (h d) -> p h d", d=DH),
                                          rec[:, r1, :].unsqueeze(2).to_broadcast([P, H, DH])).then_inc(E["recx_ready"], 1)
                if has(i, 1):
                    b, r = i + 1, (m + 1) % RING
                    after(dve, E["rs1"], b)
                    after(dve, E["xT_done"], b - 2)
                    nc.vector.tensor_scalar(xn[:, r1, :], xin[:, r, :], mv1[:, r, 0:1], rstd1[:, r:r + 1],
                                            ALU.subtract, ALU.mult).then_inc(E["xn_ready"], 1)
                if has(i, -2):
                    after(dve, E["o_done"], i - 2)
                    after(dve, E["xb_ready"], i - 2)
                    nc.vector.tensor_tensor(at(x2, i - 2), ps_a[:, 0:D], at(x2, i - 2), ALU.add).then_inc(E["x2_ready"], 1)
                if has(i, 0):
                    after(dve, E["v_done"], i)
                    after(dve, E["av_done"], i - 2)
                    nc.vector.tensor_tensor(
                        vpad[0:SK, r0, :, :].rearrange("p g (j c) -> p g j c", j=HG)[:, :, :, 0:DH],
                        ps_b[0:SK, 0:D].rearrange("p (g j c) -> p g j c", g=G, j=HG),
                        bv[0:SK, :].rearrange("p (g j c) -> p g j c", g=G, j=HG), ALU.add).then_inc(E["v_ready"], 1)
                if has(i, -2):
                    after(dve, E["x2_ready"], i - 2)
                    settled(dve)
                    nc.vector.bn_stats(st2[:, r0, :], at(x2, i - 2)).then_inc(E["bn2"], 1)
                    after(dve, E["bn2"], i - 2)
                    settled(dve)
                    nc.vector.bn_aggr(mv2[:, r0, :], st2[:, r0, :]).then_inc(E["ln2"], 1)
                if has(i, 0):
                    hs = 2 * HB
                    mxa = mx[:, r0, 0:hs].rearrange("p (n h) -> p n h", n=2)
                    after(dve, E["s01_done"], i)
                    nc.vector.tensor_reduce(mxa, bank(0, 2, HB), AX.X, ALU.max).then_inc(E["max01"], 1)
                    after(dve, E["s2_done"], i)
                    nc.vector.tensor_reduce(mx[:, r0, hs:H], bank(2, 1, H - hs), AX.X, ALU.max).then_inc(E["max2"], 1)
                    after(dve, E["max01"], i)
                    after(dve, E["t3_done"], i - 2)
                    nc.vector.tensor_tensor(pr[:, r0, 0:hs, :].rearrange("p (n h) k -> p n h k", n=2), bank(0, 2, HB),
                                            mxa.unsqueeze(3).to_broadcast([P, 2, HB, SK]), ALU.subtract).then_inc(E["sub01"], 1)
                    after(dve, E["max2"], i)
                    nc.vector.tensor_tensor(pr[:, r0, hs:H, :], bank(2, 1, H - hs).rearrange("p n h k -> p (n h) k"),
                                            mx[:, r0, hs:H].unsqueeze(2).to_broadcast([P, H - hs, SK]), ALU.subtract
                                            ).then_inc(E["sub_done"], 1)
                if has(i, -5):
                    b, r = i - 5, (m - 5) % RING
                    after(dve, E["rank_done"], b)
                    nc.vector.tensor_tensor(rk[:, :], ps_b[:, 256:256 + NE], list_base[:, 0:NE], ALU.add).then_inc(E["rk_ready"], 1)
                    after(dve, E["rk_ready"], b)
                    nc.vector.tensor_tensor(prod[:, :, :], ohs[:, r1, :, :], rk[:, :].unsqueeze(1).to_broadcast([P, TOPK, NE]),
                                            ALU.mult).then_inc(E["prod_ready"], 1)
                    after(dve, E["prod_ready"], b)
                    with nc.allow_low_precision(reason="rows are whole numbers below 2**24, summed in float32"):
                        nc.vector.tensor_reduce(slots[:, r, :], prod[:, :, :], AX.X, ALU.add).then_inc(E["slot_ready"], 1)
                if has(i, -4):
                    b = i - 4
                    after(dve, E["ginv_ready"], b)
                    after(dve, E["dots_ready"], b)
                    nc.vector.tensor_scalar(gv[:, :], dots[:, r0, :], ginv[:, r0:r0 + 1], MASKED, ALU.mult, ALU.max
                                            ).then_inc(E["gv_ready"], 1)
                    after(dve, E["gv_ready"], b)
                    settled(dve)
                    nc.vector.max(top8[:, :], gv[:, :]).then_inc(E["top_ready"], 1)
                    after(dve, E["top_ready"], b)
                    settled(dve)
                    nc.vector.max_index(idx8[:, :], top8[:, :], gv[:, :]).then_inc(E["idx_ready"], 1)
                    dcol = diff[:, b:b + 1] if known(b) else diff[:, bass.ds(b, 1)]
                    nc.vector.tensor_tensor(dcol, top8[:, 1:2], top8[:, 0:1], ALU.subtract).then_inc(E["diff_ready"], 1)
                    after(dve, E["idx_ready"], b)
                    nc.vector.tensor_tensor(ohs[:, r0, :, :], iota_e[:, 0:NE].unsqueeze(1).to_broadcast([P, TOPK, NE]),
                                            idx8[:, 0:TOPK].unsqueeze(2).to_broadcast([P, TOPK, NE]), ALU.is_equal
                                            ).then_inc(E["ohs_ready"], 1)
                    after(dve, E["ohs_ready"], b)
                    after(dve, E["rank_done"], b - 2)
                    nc.vector.tensor_tensor(sel[:, r0, :], ohs[:, r0, 0, :], ohs[:, r0, 1, :], ALU.add).then_inc(E["sel_ready"], 1)
                    after(dve, E["sel_ready"], b)
                    after(dve, E["rank_done"], b - 1)
                    after(dve, E["selsum_ready"], b - 1)
                    nc.vector.tensor_tensor(selsum[:, r1, :], selsum[:, r0, :], sel[:, r0, :], ALU.add
                                            ).then_inc(E["selsum_ready"], 1)
                if has(i, -2):
                    b, r = i - 2, (m - 2) % RING
                    after(dve, E["rs2"], b)
                    after(dve, E["xn2T_done"], b - RING)
                    after_dma(dve, scattered, b - RING, r, 16 * TOPK)
                    nc.vector.tensor_scalar(rows[:, r, :, 0:D], at(x2, b).unsqueeze(1).to_broadcast([P, TOPK, D]),
                                            mv2[:, r0, 0:1], rstd2[:, r0:r0 + 1], ALU.subtract, ALU.mult
                                            ).then_inc(E["xn2_ready"], 1)
                if has(i, 3):
                    b, r = i + 3, (m + 3) % RING
                    after_dma(dve, x_loaded, b, r)
                    settled(dve)
                    nc.vector.bn_stats(st1[:, r, :], xin[:, r, :]).then_inc(E["bn1"], 1)
                    after(dve, E["bn1"], b)
                    settled(dve)
                    nc.vector.bn_aggr(mv1[:, r, :], st1[:, r, :]).then_inc(E["ln1"], 1)
                if has(i, -1):
                    after(dve, E["av_done"], i - 1)
                    after(dve, E["recT_ready"], i - 1)
                    after(dve, E["o_done"], i - 3)
                    nc.vector.tensor_tensor(cxT[:, r1, :], ps_o[:, 0:P], recT[:, r1, :], ALU.mult).then_inc(E["cx_ready"], 1)

            steps(dve, step, -3, NB + 4, 6, NB - 4)

            n_steps = [0]

            def link(ins):
                n_steps[0] += 1
                ins.then_inc(tab_step, 1)
                dve.wait_ge(tab_step, n_steps[0])

            dve.wait_ge(cnt_done, 1)
            link(nc.vector.tensor_copy(cnt[:, :], ps_b[:, 0:NE]))
            link(nc.vector.tensor_scalar(cnti[:, :], cnt[:, :], float(P - 1), None, ALU.add))
            link(nc.vector.tensor_scalar(ntil_i[:, :], cnti[:, :], P.bit_length() - 1, None, ALU.arith_shift_right))
            link(nc.vector.tensor_copy(ntil[:, :], ntil_i[:, :]))
            link(nc.vector.tensor_tensor_scan(cum[:, :], ones8[:, :], ntil[:, :], 0.0, ALU.mult, ALU.add))
            link(nc.vector.tensor_tensor(cmp[:, :, 0:NE], iota_t[:, :].unsqueeze(2).to_broadcast([P, TT, NE]),
                                         cum[:, :].unsqueeze(1).to_broadcast([P, TT, NE]), ALU.is_ge))
            link(nc.vector.tensor_reduce(texp[:, :], cmp[:, :, 0:NE], AX.X, ALU.add))
            link(nc.vector.tensor_scalar(tmin[:, :], texp[:, :], float(NE - 1), float(F), ALU.min, ALU.mult))
            link(nc.vector.tensor_copy(tab_w[:, :], tmin[:, :]))
            link(nc.vector.tensor_scalar(tab_c[:, :], tmin[:, :], float(FC) / F, None, ALU.mult))
            link(nc.vector.tensor_scalar(tab_b[:, :], tmin[:, :], float(D) / F, None, ALU.mult))
            link(nc.vector.tensor_copy(start9[:, 0:1], list_base[:, 0:1]))
            link(nc.vector.scalar_tensor_tensor(start9[:, 1:NE + 1], cum[:, :], -float(P), list_base[:, 1:NE + 1],
                                                ALU.mult, ALU.add))
            link(nc.vector.tensor_tensor(cmp[:, :, :], texp[:, :].unsqueeze(2).to_broadcast([P, TT, NE + 1]),
                                         iota_e[:, :].unsqueeze(1).to_broadcast([P, TT, NE + 1]), ALU.is_equal))
            link(nc.vector.tensor_tensor(cmp[:, :, :], cmp[:, :, :], start9[:, :].unsqueeze(1).to_broadcast([P, TT, NE + 1]),
                                         ALU.mult))
            link(nc.vector.tensor_reduce(rbase[:, :], cmp[:, :, :], AX.X, ALU.add))
            link(nc.vector.scalar_tensor_tensor(tab_r[:, :], iota_t[:, :], float(P), rbase[:, :], ALU.mult, ALU.add))
            nc.vector.tensor_tensor(fill_r[:, :], cnt[:, :], list_base[:, 0:NE], ALU.add).then_inc(tab_ready, 1)

            dve.wait_ge(E["diff_ready"], NB)
            nc.vector.memset(den[:, :], 1.0).then_inc(p_step, 1)
            dve.wait_ge(p_exp, 1)
            dve.wait_ge(p_step, 1)
            nc.vector.tensor_tensor(den[:, :], den[:, :], expd[:, :], ALU.add).then_inc(p_step, 1)
            dve.wait_ge(p_step, 2)
            nc.vector.reciprocal(p1[:, :], den[:, :]).then_inc(p_step, 1)
            dve.wait_ge(p_step, 3)
            nc.vector.tensor_tensor(p2[:, :], expd[:, :], p1[:, :], ALU.mult).then_inc(p_step, 1)

            dve.wait_ge(tab_ready, 1)
            dve.wait_ge(wpt_copied, 2)
            dve.wait_ge(l_b2, 16)
            ps_x = [ps_a, ps_b]
            ps_e = [ps_o, ps_s[:, 2, :]]

            def entry(tab, j, top):
                return dve.value_load(tab[0:1, j:j + 1] if known(j) else tab[0:1, bass.ds(j, 1)], min_val=0, max_val=top)

            def tile(j, m):
                if has(j, 2, N_TILES):
                    r = m % 2
                    after(dve, FE["xtT_done"], j + 2)
                    after(dve, FE["up_done"], j)
                    nc.vector.tensor_copy(xtT[:, r, :], ps_x[r][:, 0:P]).then_inc(FE["xtT_ready"], 1)
                if has(j, 1, N_TILES):
                    r = (m + 1) % 2
                    e = entry(tab_c, j + 1, (NE - 1) * FC)
                    after(dve, FE["up_done"], j + 1)
                    after(dve, FE["act_ready"], j - 1)
                    nc.vector.tensor_tensor(h[:, r, :].rearrange("p (c t) -> p c t", c=FC),
                                            ps_s[:, r, :].rearrange("p (c t) -> p c t", c=FC),
                                            b1T[:, bass.ds(e, FC)].unsqueeze(2).to_broadcast([P, FC, P]), ALU.add
                                            ).then_inc(FE["h_ready"], 1)
                if has(j, -1, N_TILES):
                    r, q = (m - 1) % 2, (m - 1) % FRING
                    e = entry(tab_b, j - 1, (NE - 1) * D)
                    after(dve, FE["down_done"], j - 1)
                    after_dma(dve, returned, j - 1 - FRING, q)
                    nc.vector.tensor_tensor(eo[:, q, :], ps_e[r][:, 0:D], b2s[:, bass.ds(e, D)], ALU.add
                                            ).then_inc(FE["eo_ready"], 1)

            steps(dve, tile, -2, N_TILES, FRING + 1, N_TILES - 3, FRING)

            dve.wait_ge(p_step, 4)
            for b in range(NB):
                c, t = b // CH, b % CH
                if t == 0:
                    dve.wait_ge(y_loaded[c % 2], (c // 2 + 1) * 16 * TOPK)
                nc.vector.scalar_tensor_tensor(x2[:, b, :], ys[:, c % 2, 0, t, :], p1[:, b:b + 1], x2[:, b, :],
                                               ALU.mult, ALU.add).then_inc(sum1, 1)
                dve.wait_ge(sum1, b + 1)
                nc.vector.scalar_tensor_tensor(x2[:, b, :], ys[:, c % 2, 1, t, :], p2[:, b:b + 1], x2[:, b, :],
                                               ALU.mult, ALU.add).then_inc(sum2, 1)


_INS = ['x', 'ctx_1024', 'mask_1x1xSxS2_ik0', 'L0_xattn_W_q', 'L0_xattn_b_q', 'L0_xattn_W_k', 'L0_xattn_b_k',
        'L0_xattn_W_v', 'L0_xattn_b_v', 'L0_xattn_W_o', 'L0_xattn_b_o', 'L0_ffn_Wp', 'L0_ffn_sim_matrix',
        'L0_ffn_temperature', 'L0_ffn_W1', 'L0_ffn_b1', 'L0_ffn_W2', 'L0_ffn_b2']
_OUTS = [((32, 128, 128), 'float32')]


def kernel(**inputs):
    import numpy as _np
    import concourse.bacc as _bacc
    from concourse import mybir as _mybir
    from concourse.bass_utils import run_bass_kernel_spmd as _run

    nc = _bacc.Bacc("TRN2", target_bir_lowering=False, num_devices=1)
    arrays, args = {}, []
    for name in _INS:
        a = _np.ascontiguousarray(inputs[name])
        arrays[f"in_{name}_dram"] = a
        args.append(nc.dram_tensor(f"in_{name}_dram", a.shape, _mybir.dt.from_np(a.dtype), kind="ExternalInput").ap())
    for i, (shape, dtype) in enumerate(_OUTS):
        dt = _mybir.dt.from_np(_np.dtype(dtype))
        args.append(nc.dram_tensor(f"out_{i}_dram", shape, dt, kind="ExternalOutput").ap())
    xattn_moe_kernel(nc, *args)
    r = _run(nc, [arrays], core_ids=[0])
    got = tuple(r.results[0][f"out_{i}_dram"] for i in range(len(_OUTS)))
    return got[0]
```

```python
import concourse.bass as bass
from concourse import mybir
from contextlib import ExitStack
import math


def xattn_moe_kernel(nc, x, ctx, mask, w_q, b_q, w_k, b_k, w_v, b_v, w_o, b_o,
                     w_p, sim, temp, w1, b1, w2, b2, out):
    f32, bf16, i32, u32 = mybir.dt.float32, mybir.dt.bfloat16, mybir.dt.int32, mybir.dt.uint32
    ALU, ACT, AX = mybir.AluOpType, mybir.ActivationFunctionType, mybir.AxisListType

    NB, S, D = x.shape
    SK = ctx.shape[1]
    NE, _, F = w1.shape
    H = 16
    DH = D // H
    P = 128
    assert S == P and D == P
    NTOK = NB * S
    TOPK = 2
    G = 4
    HG = H // G
    QR = P // G
    HB = 512 // SK
    SCALE = 1.0 / math.sqrt(DH)
    MASKED = -3.0e38
    LN_EPS = 1e-5
    NORM_EPS2 = 1e-24
    FC = F // P
    REGION = NTOK + P
    N_TILES = (NTOK * TOPK + NE * (P - 1)) // P
    SPARE = N_TILES - NTOK * TOPK // P
    ROW = 132
    SKIP = 1 << 20
    RING = 4
    FRING = 8
    N_CONSTS = 15
    AHEAD = 3
    TT = N_TILES + AHEAD
    assert (NE - 1) * FC < 32

    lists = nc.dram_tensor("lists", (NE * REGION + SPARE * P, ROW), f32, kind="Internal").ap()
    results = nc.dram_tensor("results", (TOPK * NTOK, D), f32, kind="Internal").ap()

    est = ExitStack()
    with est:
        def sb(name, shape, dt=f32):
            return est.enter_context(nc.sbuf_tensor(name, shape, dt))

        def sem(name):
            return est.enter_context(nc.semaphore(name))

        identf = sb("identf", [P, P])
        identb = sb("identb", [P, P], bf16)
        tri = sb("tri", [P, P], bf16)
        onesb = sb("onesb", [P, P], bf16)
        headmask = sb("headmask", [P, H])
        headmask4 = sb("headmask4", [P, HG])
        neghalf = sb("neghalf", [P, 1])
        iota_e = sb("iota_e", [P, NE + 1])
        list_base = sb("list_base", [P, NE + 1])
        iota_t = sb("iota_t", [P, TT])
        dests = sb("dests", [P, NB, TOPK], i32)
        fill = sb("fill", [P, ROW])
        wnat = sb("wnat", [P, 5, P])
        wT = sb("wT", [P, 4, P])
        wqT, wkT, wvT, woT = (wT[:, n, :] for n in range(4))
        wg = sb("wg", [P, D + NE])
        simn = sb("simn", [NE, D])
        simd = sb("simd", [NE, D])
        simT = sb("simT", [P, NE])
        sim_sq = sb("sim_sq", [NE, D])
        sim_n2 = sb("sim_n2", [NE, 3])
        bq = sb("bq", [P, 1])
        bqs = sb("bqs", [P, 1])
        bk = sb("bk", [P, 1])
        bo_row = sb("bo_row", [P, D])
        bo = sb("bo", [P, D])
        bv = sb("bv", [P, D])
        tempc = sb("tempc", [P, 1])
        invtemp = sb("invtemp", [P, 1])
        maski = sb("maski", [P, SK], i32)
        maskn = sb("maskn", [P, SK])
        anyk = sb("anyk", [P, 3])
        negb = sb("negb", [P, HB, SK], bf16)
        w1s = sb("w1s", [P, NE * F])
        w2s = sb("w2s", [P, NE * F])
        b1n = sb("b1n", [NE * FC, P])
        b1T = sb("b1T", [P, 32 + FC])
        b2s = sb("b2s", [P, NE * D])
        xin = sb("xin", [P, RING, D])
        cin = sb("cin", [P, RING, D])
        st1 = sb("st1", [P, RING, 6])
        mv1 = sb("mv1", [P, RING, 2])
        ve1 = sb("ve1", [P, RING])
        rstd1 = sb("rstd1", [P, RING])
        xn = sb("xn", [P, 2, D])
        xT = sb("xT", [P, 2, P])
        qz = sb("qz", [P, 2, G, P])
        cT = sb("cT", [P, 2, SK])
        kT = sb("kT", [P, 2, SK])
        kbd = sb("kbd", [P, 2, HG, SK])
        vpad = sb("vpad", [P, 2, G, HG * (QR + DH)])
        mx = sb("mx", [P, 2, H])
        pr = sb("pr", [P, 2, H, SK])
        sums = sb("sums", [P, 2, H])
        rec = sb("rec", [P, 2, H])
        recx = sb("recx", [P, 2, D])
        recT = sb("recT", [P, 2, P])
        pT = sb("pT", [P, G, HG * P])
        cxT = sb("cxT", [P, 2, P])
        x2 = sb("x2", [P, NB, D])
        st2 = sb("st2", [P, 2, 6])
        mv2 = sb("mv2", [P, 2, 2])
        ve2 = sb("ve2", [P, 2])
        rstd2 = sb("rstd2", [P, 2])
        rows = sb("rows", [P, RING, TOPK, ROW])
        xn2T = sb("xn2T", [P, 2, P])
        sq_junk = sb("sq_junk", [P, D])
        n2 = sb("n2", [P, 2])
        n2c = sb("n2c", [P, 2])
        rn = sb("rn", [P, 2])
        ginv = sb("ginv", [P, 2])
        dots = sb("dots", [P, 2, NE])
        gv = sb("gv", [P, NE])
        top8 = sb("top8", [P, 8])
        idx8 = sb("idx8", [P, 8], u32)
        diff = sb("diff", [P, NB])
        ohs = sb("ohs", [P, 2, TOPK, NE])
        sel = sb("sel", [P, 2, NE], bf16)
        selsum = sb("selsum", [P, 2, NE], bf16)
        rk = sb("rk", [P, NE])
        prod = sb("prod", [P, TOPK, NE])
        slots = sb("slots", [P, RING, TOPK], i32)
        cnt = sb("cnt", [P, NE])
        cnti = sb("cnti", [P, NE], i32)
        ntil_i = sb("ntil_i", [P, NE], i32)
        ntil = sb("ntil", [P, NE])
        ones8 = sb("ones8", [P, NE])
        cum = sb("cum", [P, NE])
        start9 = sb("start9", [P, NE + 1])
        cmp = sb("cmp", [P, TT, NE + 1])
        texp = sb("texp", [P, TT])
        rbase = sb("rbase", [P, TT])
        tab_w = sb("tab_w", [P, TT], i32)
        bias_at = sb("bias_at", [P, TT])
        tab_b = sb("tab_b", [P, TT], i32)
        tab_r = sb("tab_r", [P, TT], i32)
        tmin = sb("tmin", [P, TT])
        fill_r = sb("fill_r", [P, NE], i32)
        expd = sb("expd", [P, NB])
        den = sb("den", [P, NB])
        p1 = sb("p1", [P, NB])
        p2 = sb("p2", [P, NB])
        xt = sb("xt", [P, FRING, ROW])
        w1c = sb("w1c", [P, 2, F])
        xtT = sb("xtT", [P, 2, P])
        h = sb("h", [P, 2, F])
        hT = sb("hT", [P, 2, F])
        eo = sb("eo", [P, FRING, D])
        CH = 8
        ys = sb("ys", [P, 2, TOPK, CH, D])

        ps_s = est.enter_context(nc.psum_tensor("ps_s", [P, 3, 512], f32))
        ps_t = est.enter_context(nc.psum_tensor("ps_t", [P, 2, 512], f32))
        ps_a = est.enter_context(nc.psum_tensor("ps_a", [P, 512], f32))
        ps_b = est.enter_context(nc.psum_tensor("ps_b", [P, 512], f32))
        ps_o = est.enter_context(nc.psum_tensor("ps_o", [P, 512], f32))

        l_w, l_c, l_w1, l_w2, l_b2 = (sem(n) for n in ("l_w", "l_c", "l_w1", "l_w2", "l_b2"))
        consts, filled, spare_filled = sem("consts"), sem("filled"), sem("spare_filled")
        wt_done, wt_copied, wpt_copied, simt_copied = (sem(n) for n in ("wt_done", "wt_copied", "wpt_copied", "simt_copied"))
        sim_sqd, sim_inv, sim_dir, simt_done, wgp_done, wgp_copied = (
            sem(n) for n in ("sim_sqd", "sim_inv", "sim_dir", "simt_done", "wgp_done", "wgp_copied"))
        mask_step, mask_ready, bo_ready = sem("mask_step"), sem("mask_ready"), sem("bo_ready")
        vzero, itemp, headmask4_ready, bqs_ready = (sem(n) for n in ("vzero", "itemp", "headmask4_ready", "bqs_ready"))
        x_loaded = [sem(f"x_loaded{r}") for r in range(RING)]
        c_loaded = [sem(f"c_loaded{r}") for r in range(RING)]
        scattered = [sem(f"scattered{r}") for r in range(RING)]
        names = ("bn1 ln1 var1 rs1 xn_ready xb_ready xT_done xT_ready q_done q_ready cT_done cT_ready k_done k_ready "
                 "kbd_ready v_done v_ready s0_done s1_done s2_done max0 max1 max2 sub0 sub1 exp2_done exp_done t0_done t1_done t2_done t3_done "
                 "t0_ready t1_ready t2_ready t3_ready sums_ready rec_ready recx_ready recT_done recT_ready av_done cx_ready "
                 "o_done x2_ready bn2 ln2 var2 rs2 xn2_ready dest_ready xn2T_done xn2T_ready g_done sq_ready dots_ready "
                 "n2_ready rn_ready ginv_ready gv_ready top_ready idx_ready diff_ready ohs_ready sel_ready selsum_ready "
                 "rank_done rk_ready prod_ready slot_ready").split()
        E = {n: sem(n) for n in names}
        cnt_done, tab_step, tab_ready, p_exp, p_step, exp_d = (
            sem(n) for n in ("cnt_done", "tab_step", "tab_ready", "p_exp", "p_step", "exp_d"))
        xt_loaded = [sem(f"xt_loaded{r}") for r in range(FRING)]
        returned = [sem(f"returned{r}") for r in range(FRING)]
        fnames = "xtT_done xtT_ready w1c_ready up_done h_ready act_ready down_done eo_ready".split()
        FE = {n: sem(n) for n in fnames}
        y_loaded = [sem(f"y_loaded{r}") for r in range(2)]
        sum1, sum2, stored = sem("sum1"), sem("sum2"), sem("stored")

        def known(b):
            return isinstance(b, int)

        def after(eng, s, b):
            assert known(b) or b.min_val >= 0
            if not known(b) or b >= 0:
                eng.wait_ge(s, b + 1)

        def settled(eng):
            eng.nop(nofuse=True)

        def after_dma(eng, ring, b, r, n=16):
            assert known(b) or b.min_val >= r
            if not known(b) or b >= 0:
                eng.wait_ge(ring[r], (b - r) * (n // len(ring)) + n)

        def steps(eng, step, first, last, lo, hi, body=RING):
            n = (hi - lo + 1) // body * body
            for i in range(first, lo):
                step(i, i)
            with eng.Fori(lo, lo + n - body + 1, body) as i0:
                for u in range(body):
                    step(i0 + u, lo + u)
            for i in range(lo + n, last + 1):
                step(i, i)

        def has(i, k, n=NB):
            return not known(i) or 0 <= i + k < n

        def at(ap, b):
            return ap[:, b, :] if known(b) else ap[:, bass.ds(b, 1), :].rearrange("p a n -> p (a n)")

        block = est.enter_context(nc.Block())

        @block.sync
        def _(sp):
            def step(i, m):
                b, r = i, m % RING
                if has(i, 0):
                    after(sp, E["xn_ready"], b - RING)
                    after(sp, E["xb_ready"], b - RING)
                    sp.dma_start(xin[:, r, :], x[b, :, :] if known(b) else x[bass.ds(b, 1), :, :].rearrange("a s d -> (a s) d")
                                 ).then_inc(x_loaded[r], 16)
                    after(sp, E["cT_done"], b - RING)
                    sp.dma_start(cin[0:SK, r, :], ctx[b, :, :] if known(b) else ctx[bass.ds(b, 1), :, :].rearrange("a s d -> (a s) d")
                                 ).then_inc(c_loaded[r], 16)

            steps(sp, step, 0, NB - 1, RING, NB - 1)

            sp.wait_ge(filled, 1)
            for n in range(SPARE):
                sp.dma_start(lists[NE * REGION + n * P:NE * REGION + (n + 1) * P, :], fill[:, :]).then_inc(spare_filled, 16)
            sp.wait_ge(tab_ready, 1)
            for e in range(NE):
                row = sp.value_load(fill_r[0:1, e:e + 1], min_val=e * REGION, max_val=e * REGION + NTOK)
                sp.dma_start(lists[bass.ds(row, P), :], fill[:, :]).then_inc(spare_filled, 16)
            sp.wait_ge(spare_filled, 16 * (SPARE + NE))
            for r in range(RING):
                sp.wait_ge(scattered[r], NB // RING * 16 * TOPK)

            def load_tile(j, m):
                r = m % FRING
                after(sp, FE["xtT_done"], j - FRING)
                after_dma(sp, returned, j - FRING, r)
                row = sp.value_load(tab_r[0:1, j:j + 1] if known(j) else tab_r[0:1, bass.ds(j, 1)],
                                    min_val=0, max_val=NE * REGION + (SPARE - 1) * P)
                sp.dma_start(xt[:, r, :], lists[bass.ds(row, P), :]).then_inc(xt_loaded[r], 16)

            steps(sp, load_tile, 0, N_TILES - 1, FRING, N_TILES - 1, FRING)

            for r in range(FRING):
                sp.wait_ge(returned[r], len(range(r, N_TILES, FRING)) * 16)
            res = results.rearrange("(k c t p) d -> c k p t d", k=TOPK, t=CH, p=P)
            for c in range(NB // CH):
                if c >= 2:
                    sp.wait_ge(sum2, CH * (c - 1))
                for k in range(TOPK):
                    sp.dma_start(ys[:, c % 2, k, :, :], res[c, k]).then_inc(y_loaded[c % 2], 16)
            for c in range(NB // CH):
                sp.wait_ge(sum2, CH * (c + 1))
                sp.dma_start(out[c * CH:(c + 1) * CH, :, :].rearrange("t p d -> p t d"), x2[:, c * CH:(c + 1) * CH, :]
                             ).then_inc(stored, 16)
            sp.wait_ge(stored, 16 * (NB // CH))

        @block.gpsimd
        def _(pool):
            nc.gpsimd.memset(identf[:, :], 0.0).then_inc(consts, 1)
            nc.gpsimd.memset(onesb[:, :], 1.0).then_inc(consts, 1)
            nc.gpsimd.memset(headmask[:, :], 1.0).then_inc(consts, 1)
            nc.gpsimd.memset(neghalf[:, :], -0.5).then_inc(consts, 1)
            nc.gpsimd.memset(fill[:, :], 0.0).then_inc(consts, 1)
            nc.gpsimd.memset(selsum[:, 0, :], 0.0).then_inc(consts, 1)
            pool.wait_ge(consts, 6)
            nc.gpsimd.affine_select(out=identf[:, :], in_=identf[:, :], compare_op=ALU.not_equal, fill=1.0, base=0,
                                    pattern=[[-1, P]], channel_multiplier=1).then_inc(consts, 1)
            nc.gpsimd.affine_select(out=tri[:, :], in_=onesb[:, :], compare_op=ALU.is_gt, fill=0.0, base=0,
                                    pattern=[[1, P]], channel_multiplier=-1).then_inc(consts, 1)
            nc.gpsimd.affine_select(out=headmask[:, :], in_=headmask[:, :], compare_op=ALU.is_ge, fill=0.0, base=0,
                                    pattern=[[-DH, H]], channel_multiplier=1).then_inc(consts, 1)
            pool.wait_ge(consts, 9)
            nc.gpsimd.affine_select(out=headmask[:, :], in_=headmask[:, :], compare_op=ALU.is_ge, fill=0.0, base=DH - 1,
                                    pattern=[[DH, H]], channel_multiplier=-1).then_inc(consts, 1)
            nc.gpsimd.tensor_copy(identb[:, :], identf[:, :]).then_inc(consts, 1)
            nc.gpsimd.iota(iota_e[:, :], [[1, NE + 1]], base=0, channel_multiplier=0,
                           allow_small_or_imprecise_dtypes=True).then_inc(consts, 1)
            nc.gpsimd.iota(list_base[:, :], [[REGION, NE + 1]], base=0, channel_multiplier=0,
                           allow_small_or_imprecise_dtypes=True).then_inc(consts, 1)
            nc.gpsimd.iota(iota_t[:, :], [[1, TT]], base=0, channel_multiplier=0,
                           allow_small_or_imprecise_dtypes=True).then_inc(consts, 1)
            nc.gpsimd.iota(dests[:, :, :], [[P, NB], [NTOK, TOPK]], base=0, channel_multiplier=1).then_inc(consts, 1)
            nc.gpsimd.iota(fill[:, D:D + 1].bitcast(i32), [[1, 1]], base=SKIP, channel_multiplier=0).then_inc(filled, 1)
            pool.wait_ge(consts, N_CONSTS)

            pool.wait_ge(sim_sqd, 1)
            nc.gpsimd.tensor_scalar(sim_n2[:, 1:2], sim_n2[:, 0:1], NORM_EPS2, 1.0, ALU.max, ALU.mult).then_inc(sim_inv, 1)
            pool.wait_ge(sim_inv, 1)
            nc.gpsimd.tensor_tensor(sim_n2[:, 2:3], sim_n2[:, 1:2], neghalf[0:NE, :], ALU.pow).then_inc(sim_inv, 1)
            pool.wait_ge(vzero, 3)
            pool.wait_ge(bo_ready, 1)
            pool.wait_ge(itemp, 1)

            pool.wait_ge(headmask4_ready, 1)

            def step(i, m):
                if has(i, 2):
                    b, r = i + 2, (m + 2) % RING
                    after(pool, E["ln1"], b)
                    settled(pool)
                    nc.gpsimd.tensor_scalar(ve1[:, r:r + 1], mv1[:, r, 1:2], LN_EPS, 1.0, ALU.add, ALU.mult).then_inc(E["var1"], 1)
                    after(pool, E["var1"], b)
                    after(pool, E["xn_ready"], b - RING)
                    nc.gpsimd.tensor_tensor(rstd1[:, r:r + 1], ve1[:, r:r + 1], neghalf[:, :], ALU.pow).then_inc(E["rs1"], 1)
                if has(i, -4):
                    b, r = i - 4, (m - 4) % 2
                    after(pool, E["sq_ready"], b)
                    settled(pool)
                    nc.gpsimd.tensor_scalar(n2c[:, r:r + 1], n2[:, r:r + 1], NORM_EPS2, 1.0, ALU.max, ALU.mult
                                            ).then_inc(E["n2_ready"], 1)
                    after(pool, E["n2_ready"], b)
                    nc.gpsimd.tensor_tensor(rn[:, r:r + 1], n2c[:, r:r + 1], neghalf[:, :], ALU.pow).then_inc(E["rn_ready"], 1)
                    after(pool, E["rn_ready"], b)
                    after(pool, E["gv_ready"], b - 2)
                    nc.gpsimd.tensor_tensor(ginv[:, r:r + 1], rn[:, r:r + 1], invtemp[:, :], ALU.mult
                                            ).then_inc(E["ginv_ready"], 1)
                if has(i, -5):
                    b, r = i - 5, (m - 5) % RING
                    after(pool, E["dest_ready"], b)
                    after(pool, E["xn2_ready"], b)
                    after(pool, E["slot_ready"], b)
                    settled(pool)
                    for k in range(TOPK):
                        nc.gpsimd.indirect_dma_start(lists, bass.IndirectOffsetOnAxis(ap=slots[:, r, k:k + 1], axis=0),
                                                     rows[:, r, k, :], None).then_inc(scattered[r], 16)
                if has(i, -2):
                    b, r = i - 2, (m - 2) % 2
                    after(pool, E["ln2"], b)
                    settled(pool)
                    nc.gpsimd.tensor_scalar(ve2[:, r:r + 1], mv2[:, r, 1:2], LN_EPS, 1.0, ALU.add, ALU.mult).then_inc(E["var2"], 1)
                    after(pool, E["var2"], b)
                    after(pool, E["xn2_ready"], b - 2)
                    nc.gpsimd.tensor_tensor(rstd2[:, r:r + 1], ve2[:, r:r + 1], neghalf[:, :], ALU.pow).then_inc(E["rs2"], 1)
                    r = (m - 2) % RING
                    after_dma(pool, scattered, b - RING, r, 16 * TOPK)
                    settled(pool)
                    d = dests[:, b, :] if known(b) else dests[:, bass.ds(b, 1), :].rearrange("p a n -> p (a n)")
                    nc.gpsimd.tensor_copy(rows[:, r, :, D:D + 1].rearrange("p k o -> p (k o)").bitcast(i32), d
                                          ).then_inc(E["dest_ready"], 1)
                if has(i, 1):
                    b, r = i + 1, (m + 1) % RING
                    after_dma(pool, x_loaded, b, r)
                    nc.gpsimd.tensor_tensor(at(x2, b), xin[:, r, :], bo[:, :], ALU.add).then_inc(E["xb_ready"], 1)
                if has(i, 2):
                    b, r = i + 2, (m + 2) % 2
                    after(pool, E["k_ready"], b)
                    after(pool, E["s1_done"], b - 2)
                    nc.gpsimd.tensor_tensor(kbd[:, r, :, :], kT[:, r, :].unsqueeze(1).to_broadcast([P, HG, SK]),
                                            headmask4[:, :].unsqueeze(2).to_broadcast([P, HG, SK]), ALU.mult
                                            ).then_inc(E["kbd_ready"], 1)

            steps(pool, step, -2, NB + 4, 6, NB - 3)

            def give_back(j, m):
                r = m % FRING
                after(pool, FE["eo_ready"], j)
                settled(pool)
                nc.gpsimd.indirect_dma_start(results, bass.IndirectOffsetOnAxis(ap=xt[:, r, D:D + 1].bitcast(i32), axis=0),
                                             eo[:, r, :], None, bounds_check=TOPK * NTOK - 1, oob_is_err=False
                                             ).then_inc(returned[r], 16)

            steps(pool, give_back, 0, N_TILES - 1, 0, N_TILES - 1, FRING)

        @block.tensor
        def _(pe):
            pe.wait_ge(l_w, 16 * 7)
            pe.wait_ge(consts, N_CONSTS)
            for n in range(4):
                last = nc.tensor.transpose(ps_t[:, 0, n * P:(n + 1) * P], wnat[:, n, :], identf[:, :])
            last.then_inc(wt_done, 1)
            nc.tensor.transpose(ps_t[:, 1, 0:P], wnat[:, 4, :], identf[:, :])
            nc.tensor.transpose(ps_t[:, 1, P:P + NE * FC], b1n[:, :], identf[0:NE * FC, 0:NE * FC]).then_inc(wt_done, 1)
            pe.wait_ge(sim_dir, 1)
            nc.tensor.transpose(ps_a[:, 0:NE], simd[:, :], identf[0:NE, 0:NE]).then_inc(simt_done, 1)
            pe.wait_ge(simt_copied, 1)
            nc.tensor.matmul(ps_b[:, 0:NE], wnat[:, 4, :], simT[:, :], start=True, stop=True).then_inc(wgp_done, 1)
            pe.wait_ge(wt_copied, 1)
            pe.wait_ge(wpt_copied, 2)
            pe.wait_ge(wgp_copied, 1)
            pe.wait_ge(mask_ready, 1)

            def scores(r, bank, first=True, last=True):
                h0, nh = bank * HB, min(HB, H - bank * HB)
                groups = range(h0 // HG, (h0 + nh - 1) // HG + 1)
                if first:
                    nc.tensor.matmul(ps_s[:, bank, 0:nh * SK], identb[:, :], negb[:, 0:nh, :].rearrange("p h k -> p (h k)"),
                                     start=True, stop=False)
                for g in groups[0 if first else 1:len(groups) if last else 1]:
                    a, z = max(h0, g * HG), min(h0 + nh, (g + 1) * HG)
                    done = nc.tensor.matmul(ps_s[:, bank, (a - h0) * SK:(z - h0) * SK], qz[:, r, g, :],
                                            kbd[:, r, a - g * HG:z - g * HG, :].rearrange("p h k -> p (h k)"),
                                            start=False, stop=(g == groups[-1]))
                return done

            def probs_T(b, m, g):
                r = m % 2
                for j in range(HG):
                    last = nc.tensor.transpose(ps_t[0:SK, g % 2, j * P:(j + 1) * P], pr[:, r, g * HG + j, :], identf[:, :])
                last.then_inc(E[f"t{g}_done"], 1)

            def step(i, m):
                r0, r1 = m % 2, (m + 1) % 2
                if has(i, 0):
                    after(pe, E["q_ready"], i)
                    after(pe, E["kbd_ready"], i)
                    after(pe, E["exp2_done"], i - 1)
                    scores(r0, 2).then_inc(E["s2_done"], 1)
                if has(i, -2):
                    after(pe, E["cx_ready"], i - 2)
                    if not has(i, 0):
                        after(pe, E["q_ready"], NB - 1)
                    nc.tensor.matmul(ps_a[:, 0:D], cxT[:, r0, :], woT, start=True, stop=True).then_inc(E["o_done"], 1)
                if has(i, 0):
                    after(pe, E["dots_ready"], i - 4)
                    if not has(i, -4):
                        after(pe, E["k_ready"], i + 1)
                    nc.tensor.matmul(ps_b[0:SK, 0:D], cT[:, r0, :], wvT, start=True, stop=True).then_inc(E["v_done"], 1)
                    after(pe, E["sub0"], i - 1)
                    scores(r0, 0).then_inc(E["s0_done"], 1)
                if has(i, 1):
                    after(pe, E["xn_ready"], i + 1)
                    after(pe, E["x2_ready"], i - 2)
                    if not has(i, -2):
                        after(pe, E["q_ready"], i)
                    nc.tensor.transpose(ps_a[:, 0:P], xn[:, r1, :], identf[:, :]).then_inc(E["xT_done"], 1)
                if has(i, 2):
                    after_dma(pe, c_loaded, i + 2, (m + 2) % RING)
                    after(pe, E["v_ready"], i)
                    if not has(i, 0):
                        after(pe, E["k_ready"], i + 1)
                    nc.tensor.transpose(ps_b[:, 0:SK], cin[0:SK, (m + 2) % RING, :], identf[0:SK, 0:SK]).then_inc(E["cT_done"], 1)
                if has(i, -1):
                    after(pe, E["exp_done"], i - 1)
                    probs_T(i - 1, r1, 0)
                    probs_T(i - 1, r1, 1)
                if has(i, 0):
                    after(pe, E["sub1"], i - 1)
                    scores(r0, 1, last=False)
                if has(i, -3):
                    after(pe, E["xn2_ready"], i - 3)
                    if has(i, 1):
                        after(pe, E["xT_ready"], i + 1)
                    elif has(i, -2):
                        after(pe, E["x2_ready"], i - 2)
                    else:
                        after(pe, E["xn2T_ready"], i - 4)
                    nc.tensor.transpose(ps_a[:, 0:P], rows[:, (m - 3) % RING, 0, 0:D], identf[:, :]).then_inc(E["xn2T_done"], 1)
                if has(i, 2):
                    after(pe, E["cT_ready"], i + 2)
                    nc.tensor.matmul(ps_b[:, 0:SK], wkT, cT[:, r0, :], start=True, stop=True).then_inc(E["k_done"], 1)
                if has(i, -1):
                    after(pe, E["recx_ready"], i - 1)
                    after(pe, E["rk_ready"], i - 5)
                    nc.tensor.transpose(ps_o[:, P:2 * P], recx[:, r1, :], identf[:, :]).then_inc(E["recT_done"], 1)
                    after(pe, E["t0_ready"], i - 1)
                    probs_T(i - 1, r1, 2)
                    after(pe, E["t1_ready"], i - 1)
                    probs_T(i - 1, r1, 3)
                if has(i, 0):
                    scores(r0, 1, first=False).then_inc(E["s1_done"], 1)
                if has(i, 1):
                    if not has(i, -3):
                        after(pe, E["xT_ready"], i + 1)
                    after(pe, E["xn2T_ready"], i - 3)
                    nc.tensor.matmul(ps_a[:, 0:P], wqT, xT[:, r1, :], start=True, stop=True).then_inc(E["q_done"], 1)
                if has(i, -3):
                    if not has(i, 1):
                        after(pe, E["xn2T_ready"], i - 3)
                    if has(i, 2):
                        after(pe, E["k_ready"], i + 2)
                    elif has(i, 0):
                        after(pe, E["v_ready"], i)
                    else:
                        after(pe, E["dots_ready"], i - 4)
                    nc.tensor.matmul(ps_b[:, 0:D + NE], xn2T[:, r1, :], wg[:, :], start=True, stop=True).then_inc(E["g_done"], 1)
                if has(i, -4):
                    after(pe, E["sel_ready"], i - 4)
                    after(pe, E["selsum_ready"], i - 5)
                    if has(i, -1):
                        after(pe, E["recT_ready"], i - 1)
                    else:
                        after(pe, E["cx_ready"], min(i - 2, NB - 1))
                        after(pe, E["rk_ready"], i - 5)
                    nc.tensor.matmul(ps_o[:, 256:256 + NE], tri[:, :], sel[:, r0, :], start=True, stop=False)
                    nc.tensor.matmul(ps_o[:, 256:256 + NE], onesb[:, :], selsum[:, r0, :], start=False, stop=True
                                     ).then_inc(E["rank_done"], 1)
                if has(i, -1):
                    after(pe, E["t3_ready"], i - 1)
                    if not has(i, 1):
                        after(pe, E["v_ready"], i - 1)
                    if not has(i, -4):
                        after(pe, E["recT_ready"], i - 1)
                    for j in range(HG):
                        for g in range(G):
                            last = nc.tensor.matmul(ps_o[g * QR:(g + 1) * QR, 0:P], vpad[0:SK, r1, g, j * QR:(j + 1) * QR],
                                                    pT[0:SK, g, j * P:(j + 1) * P], start=(j == 0), stop=(j == HG - 1),
                                                    tile_position=(0, g * QR))
                    last.then_inc(E["av_done"], 1)

            steps(pe, step, -2, NB + 3, 5, NB - 3)

            after(pe, E["selsum_ready"], NB - 1)
            after(pe, E["rk_ready"], NB - 1)
            nc.tensor.matmul(ps_b[:, 0:NE], onesb[:, :], selsum[:, NB % 2, :], start=True, stop=True).then_inc(cnt_done, 1)

            pe.wait_ge(l_w2, 16)
            pe.wait_ge(tab_ready, 1)
            ps_x = [ps_a, ps_b]
            ps_e = [ps_o, ps_s[:, 2, :]]

            def tile(j, m):
                if has(j, 2, N_TILES):
                    r, q = m % 2, (m + 2) % FRING
                    after_dma(pe, xt_loaded, j + 2, q)
                    after(pe, FE["xtT_ready"], j)
                    nc.tensor.transpose(ps_x[r][:, 0:P], xt[:, q, 0:D], identf[:, :]).then_inc(FE["xtT_done"], 1)
                if has(j, 1, N_TILES):
                    r = (m + 1) % 2
                    after(pe, FE["xtT_ready"], j + 1)
                    after(pe, FE["w1c_ready"], j + 1)
                    after(pe, FE["h_ready"], j - 1)
                    for c in range(FC):
                        last = nc.tensor.matmul(ps_s[:, r, c * P:(c + 1) * P], w1c[:, r, c * P:(c + 1) * P], xtT[:, r, :],
                                                start=True, stop=True)
                    last.then_inc(FE["up_done"], 1)
                if has(j, -1, N_TILES):
                    r = (m - 1) % 2
                    b = j - 1
                    e = pe.value_load(tab_w[0:1, b:b + 1] if known(b) else tab_w[0:1, bass.ds(b, 1)],
                                      min_val=0, max_val=(NE - 1) * F)
                    after(pe, FE["act_ready"], j - 1)
                    after(pe, FE["eo_ready"], j - 3)
                    for c in range(FC):
                        last = nc.tensor.matmul(ps_e[r][:, 0:D], hT[:, r, c * P:(c + 1) * P], w2s[:, bass.ds(e + c * D, D)],
                                                start=(c == 0), stop=(c == FC - 1))
                    last.then_inc(FE["down_done"], 1)

            steps(pe, tile, -2, N_TILES, 3, N_TILES - 3, FRING)

        @block.scalar
        def _(act):
            for n, w in enumerate((w_q, w_k, w_v, w_o, w_p)):
                act.dma_start(wnat[:, n, :], w).then_inc(l_w, 16)
            act.dma_start(simn[:, :], sim).then_inc(l_w, 16)
            act.dma_start(b1n[:, :], b1.rearrange("e (c f) -> (e c) f", f=P)).then_inc(l_w, 16)
            act.dma_start(bq[:, :], b_q.rearrange("(p o) -> p o", o=1)).then_inc(l_c, 16)
            act.dma_start(bk[:, :], b_k.rearrange("(p o) -> p o", o=1)).then_inc(l_c, 16)
            act.dma_start(maski[:, :], mask.rearrange("a b q k -> (a b q) k")).then_inc(l_c, 16)
            act.dma_start(bo_row[:, :], b_o.partition_broadcast(P)).then_inc(l_c, 16)
            act.dma_start(bv[:, :], b_v.partition_broadcast(P)).then_inc(l_c, 16)
            act.dma_start(tempc[:, :], temp.partition_broadcast(P)).then_inc(l_c, 16)
            act.dma_start(w1s[:, :].rearrange("p (e f) -> p e f", e=NE), w1.rearrange("e d f -> d e f")).then_inc(l_w1, 16)
            act.dma_start(w2s[:, :].rearrange("p (e c d) -> p e c d", e=NE, c=FC),
                          w2.rearrange("e (c p) d -> p e c d", p=P)).then_inc(l_w2, 16)
            act.dma_start(b2s[:, :], b2.rearrange("e d -> (e d)").partition_broadcast(P)).then_inc(l_b2, 16)
            act.wait_ge(l_w, 16 * 7)
            nc.scalar.activation(sim_sq[:, :], simn[:, :], ACT.Square, accum_out=sim_n2[:, 0:1]).then_inc(sim_sqd, 1)
            act.wait_ge(sim_inv, 2)
            nc.scalar.activation(simd[:, :], simn[:, :], ACT.Copy, scale=sim_n2[:, 2:3]).then_inc(sim_dir, 1)
            act.wait_ge(wt_done, 1)
            nc.scalar.activation(wT[:, :, :].rearrange("p n m -> p (n m)"), ps_t[:, 0, :], ACT.Copy).then_inc(wt_copied, 1)
            act.wait_ge(wt_done, 2)
            nc.scalar.activation(wg[:, 0:D], ps_t[:, 1, 0:P], ACT.Copy).then_inc(wpt_copied, 1)
            nc.scalar.activation(b1T[:, 0:NE * FC], ps_t[:, 1, P:P + NE * FC], ACT.Copy).then_inc(wpt_copied, 1)
            act.wait_ge(simt_done, 1)
            nc.scalar.activation(simT[:, :], ps_a[:, 0:NE], ACT.Copy).then_inc(simt_copied, 1)
            act.wait_ge(wgp_done, 1)
            nc.scalar.activation(wg[:, D:D + NE], ps_b[:, 0:NE], ACT.Copy).then_inc(wgp_copied, 1)
            act.wait_ge(l_c, 16 * 6)
            act.wait_ge(vzero, 4)
            act.wait_ge(bqs_ready, 1)

            def probs_out(i, g):
                after(act, E[f"t{g}_done"], i - 1)
                after(act, E["av_done"], i - 2)
                nc.scalar.activation(pT[0:SK, g, :], ps_t[0:SK, g % 2, :], ACT.Copy).then_inc(E[f"t{g}_ready"], 1)

            def step(i, m):
                r0, r1 = m % 2, (m + 1) % 2
                if has(i, -4):
                    after(act, E["g_done"], i - 4)
                    after(act, E["ginv_ready"], i - 6)
                    after(act, E["sq_ready"], i - 5)
                    nc.scalar.activation(sq_junk[:, :], ps_b[:, 0:D], ACT.Square, accum_out=n2[:, r0:r0 + 1]
                                         ).then_inc(E["sq_ready"], 1)
                    after(act, E["gv_ready"], i - 6)
                    nc.scalar.activation(dots[:, r0, :], ps_b[:, D:D + NE], ACT.Copy).then_inc(E["dots_ready"], 1)
                if has(i, 0):
                    after(act, E["t3_done"], i - 2)
                    after(act, E["rec_ready"], i - 2)
                    after(act, E["max2"], i)
                    for hd in range(2 * HB, H):
                        c = (hd - 2 * HB) * SK
                        last = nc.scalar.activation(pr[:, r0, hd, :], ps_s[:, 2, c:c + SK], ACT.Exp, bias=mx[:, r0, hd:hd + 1],
                                                    accum_out=sums[:, r0, hd:hd + 1])
                    last.then_inc(E["exp2_done"], 1)
                if has(i, 1):
                    after(act, E["xT_done"], i + 1)
                    after(act, E["q_done"], i - 1)
                    nc.scalar.activation(xT[:, r1, :], ps_a[:, 0:P], ACT.Copy).then_inc(E["xT_ready"], 1)
                if has(i, 2):
                    after(act, E["cT_done"], i + 2)
                    after(act, E["v_done"], i)
                    after(act, E["k_done"], i)
                    nc.scalar.activation(cT[:, r0, :], ps_b[:, 0:SK], ACT.Copy).then_inc(E["cT_ready"], 1)
                if has(i, -1):
                    probs_out(i, 0)
                    probs_out(i, 1)
                if has(i, -3):
                    after(act, E["xn2T_done"], i - 3)
                    after(act, E["g_done"], i - 5)
                    nc.scalar.activation(xn2T[:, r1, :], ps_a[:, 0:P], ACT.Copy).then_inc(E["xn2T_ready"], 1)
                if has(i, 2):
                    after(act, E["k_done"], i + 2)
                    after(act, E["kbd_ready"], i)
                    nc.scalar.activation(kT[:, r0, :], ps_b[:, 0:SK], ACT.Identity, bias=bk[:, 0:1]).then_inc(E["k_ready"], 1)
                if has(i, -1):
                    after(act, E["recT_done"], i - 1)
                    after(act, E["cx_ready"], i - 3)
                    nc.scalar.activation(recT[:, r1, :], ps_o[:, P:2 * P], ACT.Copy).then_inc(E["recT_ready"], 1)
                    probs_out(i, 2)
                    probs_out(i, 3)
                if has(i, 1):
                    after(act, E["q_done"], i + 1)
                    after(act, E["s1_done"], i - 1)
                    for g in range(G):
                        rws = slice(g * QR, (g + 1) * QR)
                        last = nc.scalar.activation(qz[rws, r1, g, :], ps_a[rws, 0:P], ACT.Identity, bias=bqs[rws, 0:1], scale=SCALE)
                    last.then_inc(E["q_ready"], 1)
                if has(i, 0):
                    after(act, E["sub1"], i)
                    p = pr[:, r0, 0:2 * HB, :].rearrange("p h k -> p (h k)")
                    nc.scalar.activation(p, p, ACT.Exp).then_inc(E["exp_done"], 1)

            steps(act, step, -2, NB + 3, 6, NB - 3)

            act.wait_ge(p_step, 0 + 1)
            nc.scalar.activation(expd[:, :], diff[:, :], ACT.Exp).then_inc(p_exp, 1)

            act.wait_ge(l_w1, 16)
            act.wait_ge(tab_ready, 1)

            def tile(j, m):
                r = m % 2
                if has(j, 2, N_TILES):
                    b = j + 2
                    e = act.value_load(tab_w[0:1, b:b + 1] if known(b) else tab_w[0:1, bass.ds(b, 1)],
                                       min_val=0, max_val=(NE - 1) * F)
                    after(act, FE["up_done"], j)
                    settled(act)
                    nc.scalar.activation(w1c[:, r, :], w1s[:, bass.ds(e, F)], ACT.Copy).then_inc(FE["w1c_ready"], 1)
                if has(j, 0, N_TILES):
                    after(act, FE["h_ready"], j)
                    after(act, FE["down_done"], j - 2)
                    nc.scalar.activation(hT[:, r, :], h[:, r, :], ACT.Gelu).then_inc(FE["act_ready"], 1)

            steps(act, tile, -2, N_TILES - 1, 2, N_TILES - 3, FRING)

        @block.vector
        def _(dve):
            nc.vector.memset(vpad[:, :, :, :], 0.0).then_inc(vzero, 1)
            nc.vector.memset(ones8[:, :], 1.0).then_inc(vzero, 1)
            nc.vector.memset(rows[:, :, :, :], 0.0).then_inc(vzero, 1)
            nc.vector.memset(qz[:, :, :, :], 0.0).then_inc(vzero, 1)
            dve.wait_ge(vzero, 4)
            dve.wait_ge(l_c, 16 * 6)
            dve.wait_ge(consts, N_CONSTS)
            nc.vector.tensor_reduce(headmask4[:, :], headmask[:, :].rearrange("p (g j) -> p j g", g=G), AX.X, ALU.add
                                    ).then_inc(headmask4_ready, 1)
            nc.vector.tensor_scalar(bqs[:, :], bq[:, :], SCALE, None, ALU.mult).then_inc(bqs_ready, 1)
            nc.vector.reciprocal(invtemp[:, :], tempc[:, :]).then_inc(itemp, 1)
            nc.vector.tensor_scalar(negb[:, :, :], maski[:, :].unsqueeze(1).to_broadcast([P, HB, SK]), 0.0, MASKED,
                                    ALU.is_equal, ALU.mult).then_inc(mask_ready, 1)
            nc.vector.tensor_scalar(maskn[:, :], maski[:, :], 0.0, None, ALU.not_equal).then_inc(mask_step, 1)
            dve.wait_ge(mask_step, 1)
            nc.vector.tensor_reduce(anyk[:, 0:1], maskn[:, :], AX.X, ALU.max).then_inc(mask_step, 1)
            dve.wait_ge(mask_step, 2)
            nc.vector.reciprocal(anyk[:, 1:2], anyk[:, 0:1]).then_inc(mask_step, 1)
            dve.wait_ge(mask_step, 3)
            nc.vector.tensor_scalar(anyk[:, 2:3], anyk[:, 1:2], 0.0, None, ALU.mult).then_inc(mask_step, 1)
            dve.wait_ge(mask_step, 4)
            nc.vector.tensor_scalar(bo[:, :], bo_row[:, :], anyk[:, 2:3], None, ALU.add).then_inc(bo_ready, 1)

            def bank(n, nh):
                return ps_s[:, n, 0:nh * SK].rearrange("p (h k) -> p h k", k=SK)

            hs = 2 * HB

            def maximum(i, r, n, hd, nh):
                after(dve, E[f"s{n}_done"], i)
                nc.vector.tensor_reduce(mx[:, r, hd:hd + nh], bank(n, nh), AX.X, ALU.max, negate=True).then_inc(E[f"max{n}"], 1)

            def less_maximum(i, r, n):
                after(dve, E[f"max{n}"], i)
                after(dve, E["t3_done"], i - 2)
                hd = n * HB
                nc.vector.tensor_tensor(pr[:, r, hd:hd + HB, :], bank(n, HB), mx[:, r, hd:hd + HB].unsqueeze(2).to_broadcast([P, HB, SK]),
                                        ALU.add).then_inc(E[f"sub{n}"], 1)

            def step(i, m):
                r0, r1 = m % 2, (m + 1) % 2
                if has(i, -5):
                    after(dve, E["rk_ready"], i - 5)
                    nc.vector.tensor_tensor(prod[:, :, :], ohs[:, r1, :, :], rk[:, :].unsqueeze(1).to_broadcast([P, TOPK, NE]),
                                            ALU.mult).then_inc(E["prod_ready"], 1)
                if has(i, 0):
                    maximum(i, r0, 2, hs, H - hs)
                if has(i, -2):
                    after(dve, E["o_done"], i - 2)
                    after(dve, E["xb_ready"], i - 2)
                    nc.vector.tensor_tensor(at(x2, i - 2), ps_a[:, 0:D], at(x2, i - 2), ALU.add).then_inc(E["x2_ready"], 1)
                if has(i, 0):
                    after(dve, E["v_done"], i)
                    after(dve, E["av_done"], i - 2)
                    nc.vector.tensor_tensor(
                        vpad[0:SK, r0, :, :].rearrange("p g (j c) -> p g j c", j=HG)[:, :, :, 0:DH],
                        ps_b[0:SK, 0:D].rearrange("p (g j c) -> p g j c", g=G, j=HG),
                        bv[0:SK, :].rearrange("p (g j c) -> p g j c", g=G, j=HG), ALU.add).then_inc(E["v_ready"], 1)
                if has(i, -5):
                    b, r = i - 5, (m - 5) % RING
                    after(dve, E["prod_ready"], b)
                    with nc.allow_low_precision(reason="rows are whole numbers below 2**24, summed in float32"):
                        nc.vector.tensor_reduce(slots[:, r, :], prod[:, :, :], AX.X, ALU.add).then_inc(E["slot_ready"], 1)
                if has(i, -2):
                    after(dve, E["x2_ready"], i - 2)
                    settled(dve)
                    nc.vector.bn_stats(st2[:, r0, :], at(x2, i - 2)).then_inc(E["bn2"], 1)
                if has(i, -1):
                    after(dve, E["exp_done"], i - 1)
                    nc.vector.tensor_reduce(sums[:, r1, 0:hs], pr[:, r1, 0:hs, :], AX.X, ALU.add).then_inc(E["sums_ready"], 1)
                if has(i, -2):
                    after(dve, E["bn2"], i - 2)
                    settled(dve)
                    nc.vector.bn_aggr(mv2[:, r0, :], st2[:, r0, :]).then_inc(E["ln2"], 1)
                if has(i, -4):
                    after(dve, E["ginv_ready"], i - 4)
                    after(dve, E["dots_ready"], i - 4)
                    nc.vector.tensor_scalar(gv[:, :], dots[:, r0, :], ginv[:, r0:r0 + 1], MASKED, ALU.mult, ALU.max
                                            ).then_inc(E["gv_ready"], 1)
                if has(i, -1):
                    after(dve, E["exp2_done"], i - 1)
                    after(dve, E["sums_ready"], i - 1)
                    nc.vector.reciprocal(rec[:, r1, :], sums[:, r1, :]).then_inc(E["rec_ready"], 1)
                if has(i, 3):
                    b, r = i + 3, (m + 3) % RING
                    after_dma(dve, x_loaded, b, r)
                    settled(dve)
                    nc.vector.bn_stats(st1[:, r, :], xin[:, r, :]).then_inc(E["bn1"], 1)
                if has(i, -4):
                    after(dve, E["gv_ready"], i - 4)
                    settled(dve)
                    nc.vector.max(top8[:, :], gv[:, :]).then_inc(E["top_ready"], 1)
                if has(i, -1):
                    after(dve, E["rec_ready"], i - 1)
                    after(dve, E["recT_done"], i - 3)
                    nc.vector.tensor_copy(recx[:, r1, :].rearrange("p (h d) -> p h d", d=DH),
                                          rec[:, r1, :].unsqueeze(2).to_broadcast([P, H, DH])).then_inc(E["recx_ready"], 1)
                if has(i, 3):
                    after(dve, E["bn1"], i + 3)
                    settled(dve)
                    nc.vector.bn_aggr(mv1[:, r, :], st1[:, r, :]).then_inc(E["ln1"], 1)
                if has(i, -4):
                    after(dve, E["top_ready"], i - 4)
                    settled(dve)
                    nc.vector.max_index(idx8[:, :], top8[:, :], gv[:, :]).then_inc(E["idx_ready"], 1)
                    b = i - 4
                    dcol = diff[:, b:b + 1] if known(b) else diff[:, bass.ds(b, 1)]
                    nc.vector.tensor_tensor(dcol, top8[:, 1:2], top8[:, 0:1], ALU.subtract).then_inc(E["diff_ready"], 1)
                if has(i, 0):
                    maximum(i, r0, 0, 0, HB)
                if has(i, -4):
                    after(dve, E["idx_ready"], i - 4)
                    nc.vector.tensor_tensor(ohs[:, r0, :, :], iota_e[:, 0:NE].unsqueeze(1).to_broadcast([P, TOPK, NE]),
                                            idx8[:, 0:TOPK].unsqueeze(2).to_broadcast([P, TOPK, NE]), ALU.is_equal
                                            ).then_inc(E["ohs_ready"], 1)
                if has(i, 2):
                    r = (m + 2) % RING
                    after(dve, E["rs1"], i + 2)
                    after(dve, E["xT_done"], i)
                    nc.vector.tensor_scalar(xn[:, r0, :], xin[:, r, :], mv1[:, r, 0:1], rstd1[:, r:r + 1],
                                            ALU.subtract, ALU.mult).then_inc(E["xn_ready"], 1)
                if has(i, -4):
                    after(dve, E["ohs_ready"], i - 4)
                    after(dve, E["rank_done"], i - 6)
                    nc.vector.tensor_tensor(sel[:, r0, :], ohs[:, r0, 0, :], ohs[:, r0, 1, :], ALU.add).then_inc(E["sel_ready"], 1)
                if has(i, 0):
                    less_maximum(i, r0, 0)
                    maximum(i, r0, 1, HB, HB)
                if has(i, 0):
                    less_maximum(i, r0, 1)
                if has(i, -4):
                    after(dve, E["sel_ready"], i - 4)
                    after(dve, E["rank_done"], i - 5)
                    after(dve, E["selsum_ready"], i - 5)
                    nc.vector.tensor_tensor(selsum[:, r1, :], selsum[:, r0, :], sel[:, r0, :], ALU.add
                                            ).then_inc(E["selsum_ready"], 1)
                if has(i, -2):
                    b, r = i - 2, (m - 2) % RING
                    after(dve, E["rs2"], b)
                    after(dve, E["xn2T_done"], b - RING)
                    after_dma(dve, scattered, b - RING, r, 16 * TOPK)
                    nc.vector.tensor_scalar(rows[:, r, :, 0:D], at(x2, b).unsqueeze(1).to_broadcast([P, TOPK, D]),
                                            mv2[:, r0, 0:1], rstd2[:, r0:r0 + 1], ALU.subtract, ALU.mult
                                            ).then_inc(E["xn2_ready"], 1)
                if has(i, -1):
                    after(dve, E["recT_ready"], i - 1)
                    after(dve, E["o_done"], i - 3)
                    after(dve, E["av_done"], i - 1)
                    nc.vector.tensor_tensor(cxT[:, r1, :], ps_o[:, 0:P], recT[:, r1, :], ALU.mult).then_inc(E["cx_ready"], 1)
                if has(i, -4):
                    after(dve, E["rank_done"], i - 4)
                    nc.vector.tensor_tensor(rk[:, :], ps_o[:, 256:256 + NE], list_base[:, 0:NE], ALU.add).then_inc(E["rk_ready"], 1)

            steps(dve, step, -3, NB + 4, 6, NB - 4)

            n_steps = [0]

            def link(ins):
                n_steps[0] += 1
                ins.then_inc(tab_step, 1)
                dve.wait_ge(tab_step, n_steps[0])

            dve.wait_ge(cnt_done, 1)
            link(nc.vector.tensor_copy(cnt[:, :], ps_b[:, 0:NE]))
            link(nc.vector.tensor_scalar(cnti[:, :], cnt[:, :], float(P - 1), None, ALU.add))
            link(nc.vector.tensor_scalar(ntil_i[:, :], cnti[:, :], P.bit_length() - 1, None, ALU.arith_shift_right))
            link(nc.vector.tensor_copy(ntil[:, :], ntil_i[:, :]))
            link(nc.vector.tensor_tensor_scan(cum[:, :], ones8[:, :], ntil[:, :], 0.0, ALU.mult, ALU.add))
            link(nc.vector.tensor_tensor(cmp[:, :, 0:NE], iota_t[:, :].unsqueeze(2).to_broadcast([P, TT, NE]),
                                         cum[:, :].unsqueeze(1).to_broadcast([P, TT, NE]), ALU.is_ge))
            link(nc.vector.tensor_reduce(texp[:, :], cmp[:, :, 0:NE], AX.X, ALU.add))
            link(nc.vector.tensor_scalar(tmin[:, :], texp[:, :], float(NE - 1), float(F), ALU.min, ALU.mult))
            link(nc.vector.tensor_copy(tab_w[:, :], tmin[:, :]))
            link(nc.vector.tensor_scalar(bias_at[:, :], tmin[:, :], float(FC) / F, None, ALU.mult))
            link(nc.vector.tensor_copy(tab_b[:, 0:AHEAD], bias_at[:, 0:AHEAD]))
            link(nc.vector.scalar_tensor_tensor(tab_b[:, AHEAD:TT], bias_at[:, 0:TT - AHEAD], 32.0, bias_at[:, AHEAD:TT],
                                                ALU.mult, ALU.add))
            link(nc.vector.tensor_copy(start9[:, 0:1], list_base[:, 0:1]))
            link(nc.vector.scalar_tensor_tensor(start9[:, 1:NE + 1], cum[:, :], -float(P), list_base[:, 1:NE + 1],
                                                ALU.mult, ALU.add))
            link(nc.vector.tensor_tensor(cmp[:, :, :], texp[:, :].unsqueeze(2).to_broadcast([P, TT, NE + 1]),
                                         iota_e[:, :].unsqueeze(1).to_broadcast([P, TT, NE + 1]), ALU.is_equal))
            link(nc.vector.tensor_tensor(cmp[:, :, :], cmp[:, :, :], start9[:, :].unsqueeze(1).to_broadcast([P, TT, NE + 1]),
                                         ALU.mult))
            link(nc.vector.tensor_reduce(rbase[:, :], cmp[:, :, :], AX.X, ALU.add))
            link(nc.vector.scalar_tensor_tensor(tab_r[:, :], iota_t[:, :], float(P), rbase[:, :], ALU.mult, ALU.add))
            nc.vector.tensor_tensor(fill_r[:, :], cnt[:, :], list_base[:, 0:NE], ALU.add).then_inc(tab_ready, 1)

            dve.wait_ge(E["diff_ready"], NB)
            nc.vector.memset(den[:, :], 1.0).then_inc(p_step, 1)
            dve.wait_ge(p_exp, 1)
            dve.wait_ge(p_step, 1)
            nc.vector.tensor_tensor(den[:, :], den[:, :], expd[:, :], ALU.add).then_inc(p_step, 1)
            dve.wait_ge(p_step, 2)
            nc.vector.reciprocal(p1[:, :], den[:, :]).then_inc(p_step, 1)
            dve.wait_ge(p_step, 3)
            nc.vector.tensor_tensor(p2[:, :], expd[:, :], p1[:, :], ALU.mult).then_inc(p_step, 1)

            dve.wait_ge(tab_ready, 1)
            dve.wait_ge(wpt_copied, 2)
            dve.wait_ge(l_b2, 16)
            ps_x = [ps_a, ps_b]
            ps_e = [ps_o, ps_s[:, 2, :]]

            def tile(j, m):
                t = j - 1 + AHEAD
                if has(j, -1, N_TILES) or has(t, 0, N_TILES):
                    both = dve.value_load(tab_b[0:1, t:t + 1] if known(t) else tab_b[0:1, bass.ds(t, 1)],
                                          min_val=0, max_val=33 * (NE - 1) * FC)
                    e1, e2 = both % 32, both // 32 * (D // FC)
                if has(j, -1, N_TILES):
                    r, q = (m - 1) % 2, (m - 1) % FRING
                    after_dma(dve, returned, j - 1 - FRING, q)
                    after(dve, FE["down_done"], j - 1)
                    nc.vector.tensor_tensor(eo[:, q, :], ps_e[r][:, 0:D], b2s[:, bass.ds(e2, D)], ALU.add
                                            ).then_inc(FE["eo_ready"], 1)
                if has(j, 3, N_TILES):
                    r = (m + 1) % 2
                    after(dve, FE["up_done"], j + 1)
                    after(dve, FE["xtT_done"], j + 3)
                    nc.vector.tensor_copy(xtT[:, r, :], ps_x[r][:, 0:P]).then_inc(FE["xtT_ready"], 1)
                if has(j, 2, N_TILES):
                    r = m % 2
                    after(dve, FE["act_ready"], j)
                    after(dve, FE["up_done"], j + 2)
                    nc.vector.tensor_tensor(h[:, r, :].rearrange("p (c t) -> p c t", c=FC),
                                            ps_s[:, r, :].rearrange("p (c t) -> p c t", c=FC),
                                            b1T[:, bass.ds(e1, FC)].unsqueeze(2).to_broadcast([P, FC, P]), ALU.add
                                            ).then_inc(FE["h_ready"], 1)

            steps(dve, tile, -3, N_TILES, FRING + 1, N_TILES - 4, FRING)

            dve.wait_ge(p_step, 4)
            for b in range(NB):
                c, t = b // CH, b % CH
                if t == 0:
                    dve.wait_ge(y_loaded[c % 2], (c // 2 + 1) * 16 * TOPK)
                nc.vector.scalar_tensor_tensor(x2[:, b, :], ys[:, c % 2, 0, t, :], p1[:, b:b + 1], x2[:, b, :],
                                               ALU.mult, ALU.add).then_inc(sum1, 1)
                dve.wait_ge(sum1, b + 1)
                nc.vector.scalar_tensor_tensor(x2[:, b, :], ys[:, c % 2, 1, t, :], p2[:, b:b + 1], x2[:, b, :],
                                               ALU.mult, ALU.add).then_inc(sum2, 1)


_INS = ['x', 'ctx_1024', 'mask_1x1xSxS2_ik0', 'L0_xattn_W_q', 'L0_xattn_b_q', 'L0_xattn_W_k', 'L0_xattn_b_k',
        'L0_xattn_W_v', 'L0_xattn_b_v', 'L0_xattn_W_o', 'L0_xattn_b_o', 'L0_ffn_Wp', 'L0_ffn_sim_matrix',
        'L0_ffn_temperature', 'L0_ffn_W1', 'L0_ffn_b1', 'L0_ffn_W2', 'L0_ffn_b2']
_OUTS = [((32, 128, 128), 'float32')]


def kernel(**inputs):
    import numpy as _np
    import concourse.bacc as _bacc
    from concourse import mybir as _mybir
    from concourse.bass_utils import run_bass_kernel_spmd as _run

    nc = _bacc.Bacc("TRN2", target_bir_lowering=False, num_devices=1)
    arrays, args = {}, []
    for name in _INS:
        a = _np.ascontiguousarray(inputs[name])
        arrays[f"in_{name}_dram"] = a
        args.append(nc.dram_tensor(f"in_{name}_dram", a.shape, _mybir.dt.from_np(a.dtype), kind="ExternalInput").ap())
    for i, (shape, dtype) in enumerate(_OUTS):
        dt = _mybir.dt.from_np(_np.dtype(dtype))
        args.append(nc.dram_tensor(f"out_{i}_dram", shape, dt, kind="ExternalOutput").ap())
    xattn_moe_kernel(nc, *args)
    r = _run(nc, [arrays], core_ids=[0])
    got = tuple(r.results[0][f"out_{i}_dram"] for i in range(len(_OUTS)))
    return got[0]
```

```python
import concourse.bass as bass
from concourse import mybir
from contextlib import ExitStack
import math


def xattn_moe_kernel(nc, x, ctx, mask, w_q, b_q, w_k, b_k, w_v, b_v, w_o, b_o,
                     w_p, sim, temp, w1, b1, w2, b2, out):
    f32, bf16, i32, u32 = mybir.dt.float32, mybir.dt.bfloat16, mybir.dt.int32, mybir.dt.uint32
    ALU, ACT, AX = mybir.AluOpType, mybir.ActivationFunctionType, mybir.AxisListType

    NB, S, D = x.shape
    SK = ctx.shape[1]
    NE, _, F = w1.shape
    H = 16
    DH = D // H
    P = 128
    assert S == P and D == P
    NTOK = NB * S
    TOPK = 2
    G = 4
    HG = H // G
    QR = P // G
    HB = 512 // SK
    SCALE = 1.0 / math.sqrt(DH)
    MASKED = -3.0e38
    LN_EPS = 1e-5
    NORM_EPS2 = 1e-24
    FC = F // P
    REGION = P + NTOK
    PART = NB * 3 // 4
    N_TILES = (NTOK * TOPK + NE * (P - 1)) // P
    FULL_TILES = -(-(PART * S * TOPK - NE * (P - 1)) // P)
    PART_DONE = (PART * S * TOPK + NE * (P - 1)) // P
    PART_TILES = [FULL_TILES, N_TILES - FULL_TILES]
    ROW = 132
    SKIP = 1 << 20
    RING = 4
    FRING = 8
    N_CONSTS = 16
    AHEAD = 3
    TWO_BANKS = 6
    DRAINED = 20
    HEADS = (4, 6)
    TAB_STAGES = [n + 8 for n in HEADS]
    PTT = 64
    assert PART % 4 == 0 and max(PART_TILES) + AHEAD <= PTT
    TT = N_TILES + AHEAD
    assert (NE - 1) * FC < 32

    lists = nc.dram_tensor("lists", (NE * REGION, ROW), f32, kind="Internal").ap()
    results = nc.dram_tensor("results", (TOPK * NTOK, D), f32, kind="Internal").ap()

    est = ExitStack()
    with est:
        def sb(name, shape, dt=f32):
            return est.enter_context(nc.sbuf_tensor(name, shape, dt))

        def sem(name):
            return est.enter_context(nc.semaphore(name))

        identf = sb("identf", [P, P])
        identb = sb("identb", [P, P], bf16)
        tri = sb("tri", [P, P], bf16)
        onesb = sb("onesb", [P, P], bf16)
        headmask = sb("headmask", [P, H])
        headmask4 = sb("headmask4", [P, HG])
        neghalf = sb("neghalf", [P, 1])
        iota_e = sb("iota_e", [P, 2 * NE])
        list_base = sb("list_base", [P, 2, NE])
        iota_p = sb("iota_p", [P, 1])
        dests = sb("dests", [P, NB, TOPK], i32)
        fill = sb("fill", [P, ROW])
        wnat = sb("wnat", [P, 5, P])
        wT = sb("wT", [P, 4, P])
        wqT, wkT, wvT, woT = (wT[:, n, :] for n in range(4))
        wg = sb("wg", [P, D + NE])
        simn = sb("simn", [NE, D])
        simd = sb("simd", [NE, D])
        simT = sb("simT", [P, NE])
        sim_sq = sb("sim_sq", [NE, D])
        sim_n2 = sb("sim_n2", [NE, 3])
        bq = sb("bq", [P, 1])
        bqs = sb("bqs", [P, 1])
        bk = sb("bk", [P, 1])
        bo_row = sb("bo_row", [P, D])
        bo = sb("bo", [P, D])
        bv = sb("bv", [P, D])
        tempc = sb("tempc", [P, 1])
        invtemp = sb("invtemp", [P, 1])
        maski = sb("maski", [P, SK], i32)
        maskn = sb("maskn", [P, SK])
        anyk = sb("anyk", [P, 3])
        negb = sb("negb", [P, HB, SK], bf16)
        w1s = sb("w1s", [P, NE * F])
        w2s = sb("w2s", [P, NE * F])
        b1n = sb("b1n", [NE * FC, P])
        b1T = sb("b1T", [P, 32 + FC])
        b2s = sb("b2s", [P, NE * D])
        xin = sb("xin", [P, RING, D])
        cin = sb("cin", [P, RING, D])
        st1 = sb("st1", [P, RING, 6])
        mv1 = sb("mv1", [P, RING, 2])
        ve1 = sb("ve1", [P, RING])
        rstd1 = sb("rstd1", [P, RING])
        xn = sb("xn", [P, 2, D])
        xT = sb("xT", [P, 2, P])
        qz = sb("qz", [P, 2, G, P])
        cT = sb("cT", [P, 2, SK])
        kT = sb("kT", [P, 2, SK])
        kbd = sb("kbd", [P, 2, HG, SK])
        vpad = sb("vpad", [P, 2, G, HG * (QR + DH)])
        mx = sb("mx", [P, 2, H])
        pr = sb("pr", [P, 2, H, SK])
        sums = sb("sums", [P, 2, H])
        rec = sb("rec", [P, 2, H])
        recx = sb("recx", [P, 2, D])
        recT = sb("recT", [P, 2, P])
        pT = sb("pT", [P, G, HG * P])
        cxT = sb("cxT", [P, 2, P])
        x2 = sb("x2", [P, NB, D])
        st2 = sb("st2", [P, 2, 6])
        mv2 = sb("mv2", [P, 2, 2])
        ve2 = sb("ve2", [P, 2])
        rstd2 = sb("rstd2", [P, 2])
        rows = sb("rows", [P, RING, TOPK, ROW])
        xn2T = sb("xn2T", [P, 2, P])
        sq_junk = sb("sq_junk", [P, D])
        n2 = sb("n2", [P, 2])
        n2c = sb("n2c", [P, 2])
        rn = sb("rn", [P, 2])
        ginv = sb("ginv", [P, 2])
        dots = sb("dots", [P, 2, NE])
        gv = sb("gv", [P, NE])
        top8 = sb("top8", [P, 8])
        idx8 = sb("idx8", [P, 8], u32)
        diff = sb("diff", [P, NB])
        ohs = sb("ohs", [P, 2, TOPK, NE])
        sel = sb("sel", [P, 2, NE], bf16)
        selsum = sb("selsum", [P, 2, NE], bf16)
        rk = sb("rk", [P, NE])
        prod = sb("prod", [P, TOPK, NE])
        slots = sb("slots", [P, RING, TOPK], i32)
        cnt = sb("cnt", [P, NE])
        cnt0 = sb("cnt0", [P, NE])
        tiles_i = sb("tiles_i", [P, 2, 2, NE], i32)
        tiles0 = sb("tiles0", [P, 2, NE])
        tiles1 = sb("tiles1", [P, NE])
        done = sb("done", [P, 2 * NE])
        todo = sb("todo", [P, 2 * NE])
        cum = sb("cum", [P, 2 * NE])
        ones16 = sb("ones16", [P, 2 * NE])
        upto = sb("upto", [P, 2 * NE])
        ahead = sb("ahead", [P, 2 * NE])
        starts = sb("starts", [P, 3, 2, NE])
        cmp = sb("cmp", [P, 2 * NE])
        which = sb("which", [P, 1])
        oh_t = sb("oh_t", [P, 2 * NE])
        start_oh = sb("start_oh", [P, 3, 2 * NE])
        start = sb("start", [P, 3])
        first = sb("first", [P, 1])
        cols = sb("cols", [P, 2])
        again = sb("again", [P, P])
        skip = sb("skip", [P, TT], i32)
        didx = sb("didx", [P, FRING], i32)
        tab_w = sb("tab_w", [1, TT], i32)
        bias_at = sb("bias_at", [1, TT])
        tab_b = sb("tab_b", [1, TT], i32)
        tab_r = sb("tab_r", [1, TT], i32)
        expd = sb("expd", [P, NB])
        den = sb("den", [P, NB])
        p1 = sb("p1", [P, NB])
        p2 = sb("p2", [P, NB])
        xt = sb("xt", [P, FRING, ROW])
        w1c = sb("w1c", [P, 2, F])
        xtT = sb("xtT", [P, 2, P])
        h = sb("h", [P, 2, F])
        hT = sb("hT", [P, 2, F])
        eo = sb("eo", [P, FRING, D])
        CH = 4
        ys = sb("ys", [P, NB // CH, TOPK, CH, D])
        warm = sb("warm", [P, 1])

        def on_pool(b):
            return b % 8 in (2, 5, 7)

        def summed_before(b, pool):
            return sum(on_pool(n) == pool for n in range(b))

        ps_s = est.enter_context(nc.psum_tensor("ps_s", [P, 3, 512], f32))
        ps_t = est.enter_context(nc.psum_tensor("ps_t", [P, 2, 512], f32))
        ps_a = est.enter_context(nc.psum_tensor("ps_a", [P, 512], f32))
        ps_b = est.enter_context(nc.psum_tensor("ps_b", [P, 512], f32))
        ps_o = est.enter_context(nc.psum_tensor("ps_o", [P, 512], f32))
        tabs = [ps_o[:, 512 - (n + 1) * PTT:512 - n * PTT] for n in range(3)]

        l_w, l_sim, l_bqk, l_mask, l_rows, l_ffn = (
            sem(n) for n in ("l_w", "l_sim", "l_bqk", "l_mask", "l_rows", "l_ffn"))
        consts, filled, prefilled = sem("consts"), sem("filled"), sem("prefilled")
        wt_done, wt_copied, wpt_copied, simt_copied = (sem(n) for n in ("wt_done", "wt_copied", "wpt_copied", "simt_copied"))
        sim_sqd, sim_inv, sim_dir, simt_done, wgp_done, wgp_copied = (
            sem(n) for n in ("sim_sqd", "sim_inv", "sim_dir", "simt_done", "wgp_done", "wgp_copied"))
        mask_step, mask_ready, bo_ready = sem("mask_step"), sem("mask_ready"), sem("bo_ready")
        vzero, itemp, headmask4_ready, bqs_ready = (sem(n) for n in ("vzero", "itemp", "headmask4_ready", "bqs_ready"))
        x_loaded = [sem(f"x_loaded{r}") for r in range(RING)]
        c_loaded = [sem(f"c_loaded{r}") for r in range(RING)]
        scattered = [sem(f"scattered{r}") for r in range(RING)]
        names = ("bn1 ln1 var1 rs1 xn_ready xb_ready xT_done xT_ready q_done q_ready cT_done cT_ready k_done k_ready "
                 "kbd_ready v_done v_ready s0_done s1_done s2_done max0 max1 max2 sub0 sub1 exp2_done exp_done t0_done t1_done t2_done t3_done "
                 "t0_ready t1_ready t2_ready t3_ready sums_ready rec_ready recx_ready recT_done recT_ready av_done cx_ready "
                 "o_done x2_ready bn2 ln2 var2 rs2 xn2_ready dest_ready xn2T_done xn2T_ready g_done sq_ready dots_ready "
                 "n2_ready rn_ready ginv_ready gv_ready top_ready idx_ready diff_ready ohs_ready sel_ready selsum_ready "
                 "rank_done rk_ready prod_ready slot_ready").split()
        E = {n: sem(n) for n in names}
        cnt_done, tab_step, cols_ready, rows_ready, again_ready, again_T, skip_ready, tab_ready, p_step, bias_step = (
            sem(n) for n in ("cnt_done", "tab_step", "cols_ready", "rows_ready", "again_ready", "again_T", "skip_ready", "tab_ready", "p_step", "bias_step"))
        xt_loaded = [sem(f"xt_loaded{r}") for r in range(FRING)]
        returned = [sem(f"returned{r}") for r in range(FRING)]
        fnames = "xtT_done xtT_ready didx_ready w1c_ready up_done h_ready act_ready down_done eo_ready".split()
        FE = {n: sem(n) for n in fnames}
        y_loaded = [sem("y_loaded_part0")] + [sem(f"y_loaded{c}") for c in range(PART // CH, NB // CH)]
        sum1, sum2, weighted, pool_sum1, pool_sum2, stored = (
            sem(n) for n in ("sum1", "sum2", "weighted", "pool_sum1", "pool_sum2", "stored"))

        def after_y(eng, c):
            if c < PART // CH:
                eng.wait_ge(y_loaded[0], 16 * TOPK * (PART // CH))
            else:
                eng.wait_ge(y_loaded[c - PART // CH + 1], 16 * TOPK)

        def known(b):
            return isinstance(b, int)

        def after(eng, s, b):
            assert known(b) or b.min_val >= 0
            if not known(b) or b >= 0:
                eng.wait_ge(s, b + 1)

        def settled(eng):
            eng.nop(nofuse=True)

        def after_dma(eng, ring, b, r, n=16):
            assert known(b) or b.min_val >= r
            if not known(b) or b >= 0:
                eng.wait_ge(ring[r], (b - r) * (n // len(ring)) + n)

        def steps(eng, step, first, last, lo, hi, body=RING, between=None):
            n = (hi - lo + 1) // body * body
            for i in range(first, lo + 1):
                if between is not None:
                    between(i)
                if i < lo:
                    step(i, i)
            with eng.Fori(lo, lo + n - body + 1, body) as i0:
                for u in range(body):
                    step(i0 + u, lo + u)
            for i in range(lo + n, last + 1):
                step(i, i)

        def has(i, k, n=NB):
            return not known(i) or 0 <= i + k < n

        def at(ap, b):
            return ap[:, b, :] if known(b) else ap[:, bass.ds(b, 1), :].rearrange("p a n -> p (a n)")

        def down_bank(m):
            return ps_a if m >= TWO_BANKS and m % 2 else ps_s[:, 2, :]

        block = est.enter_context(nc.Block())

        @block.sync
        def _(sp):
            def step(i, m):
                b, r = i, m % RING
                if has(i, 0):
                    after(sp, E["xn_ready"], b - RING)
                    after(sp, E["xb_ready"], b - RING)
                    sp.dma_start(xin[:, r, :], x[b, :, :] if known(b) else x[bass.ds(b, 1), :, :].rearrange("a s d -> (a s) d")
                                 ).then_inc(x_loaded[r], 16)
                    after(sp, E["cT_done"], b - RING)
                    sp.dma_start(cin[0:SK, r, :], ctx[b, :, :] if known(b) else ctx[bass.ds(b, 1), :, :].rearrange("a s d -> (a s) d")
                                 ).then_inc(c_loaded[r], 16)

            step(0, 0)
            sp.dma_start(wnat[:, 1, :], w_k).then_inc(l_w, 16)
            sp.dma_start(wnat[:, 0, :], w_q).then_inc(l_w, 16)
            sp.dma_start(simn[:, :], sim).then_inc(l_sim, 16)
            sp.dma_start(b1n[:, :], b1.rearrange("e (c f) -> (e c) f", f=P)).then_inc(l_sim, 16)
            sp.dma_start(maski[:, :], mask.rearrange("a b q k -> (a b q) k")).then_inc(l_mask, 16)
            for b in range(1, RING):
                step(b, b)
            sp.dma_start(w1s[:, :].rearrange("p (e f) -> p e f", e=NE), w1.rearrange("e d f -> d e f")).then_inc(l_ffn, 16)
            sp.dma_start(w2s[:, :].rearrange("p (e c d) -> p e c d", e=NE, c=FC),
                          w2.rearrange("e (c p) d -> p e c d", p=P)).then_inc(l_ffn, 16)
            sp.dma_start(b2s[:, :], b2.rearrange("e d -> (e d)").partition_broadcast(P)).then_inc(l_ffn, 16)
            steps(sp, step, RING, NB - 1, RING, NB - 1)

            sp.wait_ge(filled, 1)
            for e in range(NE):
                sp.dma_start(lists[e * REGION:e * REGION + P, :], fill[:, :]).then_inc(prefilled, 16)

            def rows_are_there(part, batches):
                for r in range(RING):
                    sp.wait_ge(scattered[r], batches // RING * 16 * TOPK)
                sp.wait_ge(rows_ready, part + 1)

            sp.wait_ge(prefilled, 16 * NE)
            rows_are_there(0, PART)

            def load_tile(j, m):
                r = m % FRING
                after(sp, FE["xtT_done"], j - FRING)
                after_dma(sp, returned, j - FRING, r)
                row = sp.value_load(tab_r[0:1, j:j + 1] if known(j) else tab_r[0:1, bass.ds(j, 1)],
                                    min_val=0, max_val=NE * REGION - P)
                sp.dma_start(xt[:, r, :], lists[bass.ds(row, P), :]).then_inc(xt_loaded[r], 16)

            early = PART_TILES[0] // FRING * FRING
            steps(sp, load_tile, 0, early - 1, FRING, early - 1, FRING)
            rows_are_there(1, NB)
            res = results.rearrange("(k c t p) d -> c k p t d", k=TOPK, t=CH, p=P)

            def all_returned(tiles):
                for r in range(FRING):
                    sp.wait_ge(returned[r], len(range(r, tiles, FRING)) * 16)

            def load_results(c):
                for k in range(TOPK):
                    sp.dma_start(ys[:, c, k, :, :], res[c, k]).then_inc(y_loaded[max(0, c - PART // CH + 1)], 16)

            late = PART_DONE + FRING + 1
            steps(sp, load_tile, early, late - 1, early, late - 1, FRING)
            all_returned(PART_DONE)
            for j in range(late, max(N_TILES, late + PART // CH)):
                if j < N_TILES:
                    load_tile(j, j)
                if j < late + PART // CH:
                    load_results(j - late)
            all_returned(N_TILES)
            for c in range(PART // CH, NB // CH):
                load_results(c)
            for c in range(NB // CH):
                sp.wait_ge(sum2, summed_before(CH * (c + 1), False))
                sp.wait_ge(pool_sum2, summed_before(CH * (c + 1), True))
                sp.dma_start(out[c * CH:(c + 1) * CH, :, :].rearrange("t p d -> p t d"), x2[:, c * CH:(c + 1) * CH, :]
                             ).then_inc(stored, 16)
            sp.wait_ge(stored, 16 * (NB // CH))

        @block.gpsimd
        def _(pool):
            nc.gpsimd.memset(identf[:, :], 0.0).then_inc(consts, 1)
            nc.gpsimd.memset(onesb[:, :], 1.0).then_inc(consts, 1)
            nc.gpsimd.memset(headmask[:, :], 1.0).then_inc(consts, 1)
            nc.gpsimd.memset(neghalf[:, :], -0.5).then_inc(consts, 1)
            nc.gpsimd.memset(fill[:, :], 0.0).then_inc(consts, 1)
            nc.gpsimd.memset(selsum[:, 0, :], 0.0).then_inc(consts, 1)
            pool.wait_ge(consts, 6)
            nc.gpsimd.affine_select(out=identf[:, :], in_=identf[:, :], compare_op=ALU.not_equal, fill=1.0, base=0,
                                    pattern=[[-1, P]], channel_multiplier=1).then_inc(consts, 1)
            nc.gpsimd.affine_select(out=tri[:, :], in_=onesb[:, :], compare_op=ALU.is_gt, fill=0.0, base=0,
                                    pattern=[[1, P]], channel_multiplier=-1).then_inc(consts, 1)
            nc.gpsimd.affine_select(out=headmask[:, :], in_=headmask[:, :], compare_op=ALU.is_ge, fill=0.0, base=0,
                                    pattern=[[-DH, H]], channel_multiplier=1).then_inc(consts, 1)
            pool.wait_ge(consts, 9)
            nc.gpsimd.affine_select(out=headmask[:, :], in_=headmask[:, :], compare_op=ALU.is_ge, fill=0.0, base=DH - 1,
                                    pattern=[[DH, H]], channel_multiplier=-1).then_inc(consts, 1)
            nc.gpsimd.tensor_copy(identb[:, :], identf[:, :]).then_inc(consts, 1)
            nc.gpsimd.iota(iota_e[:, :], [[1, 2 * NE]], base=0, channel_multiplier=0,
                           allow_small_or_imprecise_dtypes=True).then_inc(consts, 1)
            nc.gpsimd.iota(starts[:, 2, :, :], [[0, 2], [F, NE]], base=0, channel_multiplier=0,
                           allow_small_or_imprecise_dtypes=True).then_inc(consts, 1)
            nc.gpsimd.iota(list_base[:, :, :], [[0, 2], [REGION, NE]], base=P, channel_multiplier=0,
                           allow_small_or_imprecise_dtypes=True).then_inc(consts, 1)
            nc.gpsimd.iota(iota_p[:, :], [[1, 1]], base=0, channel_multiplier=1,
                           allow_small_or_imprecise_dtypes=True).then_inc(consts, 1)
            nc.gpsimd.iota(dests[:, :, :], [[P, NB], [NTOK, TOPK]], base=0, channel_multiplier=1).then_inc(consts, 1)
            nc.gpsimd.iota(fill[:, D:D + 1].bitcast(i32), [[1, 1]], base=SKIP, channel_multiplier=0).then_inc(filled, 1)
            pool.wait_ge(consts, N_CONSTS)

            pool.dma_start(bv[:, :], b_v.partition_broadcast(P)).then_inc(l_rows, 16)
            pool.dma_start(bo_row[:, :], b_o.partition_broadcast(P)).then_inc(l_rows, 16)
            pool.dma_start(tempc[:, :], temp.partition_broadcast(P)).then_inc(l_rows, 16)

            pool.wait_ge(sim_sqd, 1)
            nc.gpsimd.tensor_scalar(sim_n2[:, 1:2], sim_n2[:, 0:1], NORM_EPS2, 1.0, ALU.max, ALU.mult).then_inc(sim_inv, 1)
            pool.wait_ge(sim_inv, 1)
            nc.gpsimd.tensor_tensor(sim_n2[:, 2:3], sim_n2[:, 1:2], neghalf[0:NE, :], ALU.pow).then_inc(sim_inv, 1)

            pool.wait_ge(vzero, 4)
            pool.wait_ge(headmask4_ready, 1)

            def scatter(b, n):
                r = n % RING
                after(pool, E["dest_ready"], b)
                after(pool, E["xn2_ready"], b)
                after(pool, E["slot_ready"], b)
                settled(pool)
                for k in range(TOPK):
                    nc.gpsimd.indirect_dma_start(lists, bass.IndirectOffsetOnAxis(ap=slots[:, r, k:k + 1], axis=0),
                                                 rows[:, r, k, :], None).then_inc(scattered[r], 16)

            def second_rstd(b, n):
                r = n % 2
                after(pool, E["ln2"], b)
                settled(pool)
                nc.gpsimd.tensor_scalar(ve2[:, r:r + 1], mv2[:, r, 1:2], LN_EPS, 1.0, ALU.add, ALU.mult).then_inc(E["var2"], 1)
                after(pool, E["var2"], b)
                after(pool, E["xn2_ready"], b - 2)
                nc.gpsimd.tensor_tensor(rstd2[:, r:r + 1], ve2[:, r:r + 1], neghalf[:, :], ALU.pow).then_inc(E["rs2"], 1)
                r = n % RING
                after_dma(pool, scattered, b - RING, r, 16 * TOPK)
                settled(pool)
                d = dests[:, b, :] if known(b) else dests[:, bass.ds(b, 1), :].rearrange("p a n -> p (a n)")
                nc.gpsimd.tensor_copy(rows[:, r, :, D:D + 1].rearrange("p k o -> p (k o)").bitcast(i32), d
                                      ).then_inc(E["dest_ready"], 1)

            def step(i, m):
                if has(i, 2):
                    b, r = i + 2, (m + 2) % RING
                    after(pool, E["ln1"], b)
                    settled(pool)
                    nc.gpsimd.tensor_scalar(ve1[:, r:r + 1], mv1[:, r, 1:2], LN_EPS, 1.0, ALU.add, ALU.mult).then_inc(E["var1"], 1)
                    after(pool, E["var1"], b)
                    after(pool, E["xn_ready"], b - RING)
                    nc.gpsimd.tensor_tensor(rstd1[:, r:r + 1], ve1[:, r:r + 1], neghalf[:, :], ALU.pow).then_inc(E["rs1"], 1)
                if has(i, -4):
                    b, r = i - 4, (m - 4) % 2
                    after(pool, E["sq_ready"], b)
                    settled(pool)
                    nc.gpsimd.tensor_scalar(n2c[:, r:r + 1], n2[:, r:r + 1], NORM_EPS2, 1.0, ALU.max, ALU.mult
                                            ).then_inc(E["n2_ready"], 1)
                    after(pool, E["n2_ready"], b)
                    nc.gpsimd.tensor_tensor(rn[:, r:r + 1], n2c[:, r:r + 1], neghalf[:, :], ALU.pow).then_inc(E["rn_ready"], 1)
                    after(pool, E["rn_ready"], b)
                    after(pool, E["gv_ready"], b - 2)
                    nc.gpsimd.tensor_tensor(ginv[:, r:r + 1], rn[:, r:r + 1], invtemp[:, :], ALU.mult
                                            ).then_inc(E["ginv_ready"], 1)
                last_tiles = known(i) and i >= NB
                if has(i, -5) and not last_tiles:
                    scatter(i - 5, m - 5)
                if has(i, -2):
                    second_rstd(i - 2, m - 2)
                if last_tiles and i < NB + 2:
                    scatter(i - 5, m - 5)
                if has(i, 1):
                    b, r = i + 1, (m + 1) % RING
                    after_dma(pool, x_loaded, b, r)
                    nc.gpsimd.tensor_tensor(at(x2, b), xin[:, r, :], bo[:, :], ALU.add).then_inc(E["xb_ready"], 1)
                if has(i, 2):
                    b, r = i + 2, (m + 2) % 2
                    after(pool, E["k_ready"], b)
                    after(pool, E["s1_done"], b - 2)
                    nc.gpsimd.tensor_tensor(kbd[:, r, :, :], kT[:, r, :].unsqueeze(1).to_broadcast([P, HG, SK]),
                                            headmask4[:, :].unsqueeze(2).to_broadcast([P, HG, SK]), ALU.mult
                                            ).then_inc(E["kbd_ready"], 1)

            step(-2, -2)
            pool.wait_ge(bo_ready, 1)
            pool.wait_ge(itemp, 1)
            steps(pool, step, -1, NB, 6, NB - 3)

            def give_back(j, m):
                r = m % FRING
                after_dma(pool, xt_loaded, j, r)
                after_dma(pool, returned, j - FRING, r)
                nc.gpsimd.tensor_tensor(didx[:, r:r + 1], xt[:, r, D:D + 1].bitcast(i32), skip[:, j:j + 1] if known(j) else
                                        skip[:, bass.ds(j, 1)], ALU.add).then_inc(FE["didx_ready"], 1)
                after(pool, FE["didx_ready"], j)
                after(pool, FE["eo_ready"], j)
                settled(pool)
                nc.gpsimd.indirect_dma_start(results, bass.IndirectOffsetOnAxis(ap=didx[:, r:r + 1], axis=0),
                                             eo[:, r, :], None, bounds_check=TOPK * NTOK - 1, oob_is_err=False
                                             ).then_inc(returned[r], 16)

            def between(j):
                if j == 1:
                    step(NB + 2, NB + 2)
                elif j == 6:
                    step(NB + 3, NB + 3)
                elif j in (8, 14, 20):
                    scatter(NB - 3 + (j - 8) // 6, NB - 3 + (j - 8) // 6)
                elif j == DRAINED + 11:
                    pool.wait_ge(skip_ready, 2)

            step(NB + 1, NB + 1)
            pool.wait_ge(skip_ready, 1)
            steps(pool, give_back, 0, N_TILES - 1, DRAINED + 11, N_TILES - 1, FRING, between)

            for c in range(NB // CH):
                mine = [b for b in range(c * CH, (c + 1) * CH) if on_pool(b)]
                pool.wait_ge(weighted, TOPK * summed_before(CH * (c + 1), True))
                for b in mine:
                    nc.gpsimd.tensor_tensor(x2[:, b, :], ys[:, c, 0, b % CH, :], x2[:, b, :], ALU.add).then_inc(pool_sum1, 1)
                for b in mine:
                    pool.wait_ge(pool_sum1, summed_before(b + 1, True))
                    nc.gpsimd.tensor_tensor(x2[:, b, :], ys[:, c, 1, b % CH, :], x2[:, b, :], ALU.add).then_inc(pool_sum2, 1)

        @block.tensor
        def _(pe):
            pe.wait_ge(l_w, 16 * 5)
            pe.wait_ge(consts, N_CONSTS)
            for n in range(4):
                last = nc.tensor.transpose(ps_t[:, 0, n * P:(n + 1) * P], wnat[:, n, :], identf[:, :])
            last.then_inc(wt_done, 1)
            nc.tensor.transpose(ps_t[:, 1, 0:P], wnat[:, 4, :], identf[:, :])
            pe.wait_ge(l_sim, 16 * 2)
            nc.tensor.transpose(ps_t[:, 1, P:P + NE * FC], b1n[:, :], identf[0:NE * FC, 0:NE * FC]).then_inc(wt_done, 1)
            pe.wait_ge(wt_copied, 1)

            def scores(r, bank, first=True, last=True):
                h0, nh = bank * HB, min(HB, H - bank * HB)
                groups = range(h0 // HG, (h0 + nh - 1) // HG + 1)
                if first:
                    nc.tensor.matmul(ps_s[:, bank, 0:nh * SK], identb[:, :], negb[:, 0:nh, :].rearrange("p h k -> p (h k)"),
                                     start=True, stop=False)
                for g in groups[0 if first else 1:len(groups) if last else 1]:
                    a, z = max(h0, g * HG), min(h0 + nh, (g + 1) * HG)
                    done = nc.tensor.matmul(ps_s[:, bank, (a - h0) * SK:(z - h0) * SK], qz[:, r, g, :],
                                            kbd[:, r, a - g * HG:z - g * HG, :].rearrange("p h k -> p (h k)"),
                                            start=False, stop=(g == groups[-1]))
                return done

            def probs_T(b, m, g):
                r = m % 2
                for j in range(HG):
                    last = nc.tensor.transpose(ps_t[0:SK, g % 2, j * P:(j + 1) * P], pr[:, r, g * HG + j, :], identf[:, :])
                last.then_inc(E[f"t{g}_done"], 1)

            def project(i, r0):
                after(pe, E["cx_ready"], i - 2)
                if not has(i, 0):
                    after(pe, E["q_ready"], NB - 1)
                nc.tensor.matmul(ps_a[:, 0:D], cxT[:, r0, :], woT, start=True, stop=True).then_inc(E["o_done"], 1)

            def turn(i, m):
                after(pe, E["xn2_ready"], i - 3)
                if has(i, 1):
                    after(pe, E["xT_ready"], i + 1)
                elif has(i, -2):
                    after(pe, E["x2_ready"], i - 2)
                else:
                    after(pe, E["xn2T_ready"], i - 4)
                nc.tensor.transpose(ps_a[:, 0:P], rows[:, (m - 3) % RING, 0, 0:D], identf[:, :]).then_inc(E["xn2T_done"], 1)

            def gate(i, r1):
                if not has(i, 1):
                    after(pe, E["xn2T_ready"], i - 3)
                if has(i, 2):
                    after(pe, E["k_ready"], i + 2)
                elif has(i, 0):
                    after(pe, E["v_ready"], i)
                else:
                    after(pe, E["dots_ready"], i - 4)
                nc.tensor.matmul(ps_b[:, 0:D + NE], xn2T[:, r1, :], wg[:, :], start=True, stop=True).then_inc(E["g_done"], 1)

            def rank(i, r0):
                after(pe, E["sel_ready"], i - 4)
                after(pe, E["selsum_ready"], i - 5)
                if has(i, -1):
                    after(pe, E["recT_ready"], i - 1)
                else:
                    after(pe, E["cx_ready"], min(i - 2, NB - 1))
                    after(pe, E["rk_ready"], i - 5)
                nc.tensor.matmul(ps_o[:, 256:256 + NE], tri[:, :], sel[:, r0, :], start=True, stop=False)
                last = nc.tensor.matmul(ps_o[:, 256:256 + NE], onesb[:, :], selsum[:, r0, :], start=False, stop=True)
                if known(i) and i - 4 == PART:
                    last = nc.tensor.matmul(ps_o[:, 272:272 + NE], onesb[:, :], selsum[:, r0, :], start=True, stop=True)
                last.then_inc(E["rank_done"], 1)

            def tables(part, b):
                pe.wait_ge(cols_ready, 2 * (part + 1))
                after(pe, E["rk_ready"], b)
                nc.tensor.transpose(tabs[0][0:1, :], cols[0:PTT, 0:1], identf[0:PTT, 0:PTT])
                nc.tensor.transpose(tabs[1][0:1, :], cols[0:PTT, 1:2], identf[0:PTT, 0:PTT])
                pe.wait_ge(again_ready, part + 1)
                nc.tensor.matmul(tabs[2], again[:, :], identf[:, 0:PTT], start=True, stop=True).then_inc(again_T, 1)

            def step(i, m):
                r0, r1 = m % 2, (m + 1) % 2
                if has(i, 0):
                    after(pe, E["q_ready"], i)
                    after(pe, E["kbd_ready"], i)
                    after(pe, E["exp2_done"], i - 1)
                    scores(r0, 2).then_inc(E["s2_done"], 1)
                if has(i, -2):
                    project(i, r0)
                if known(i) and i == NB - 1:
                    tables(0, i - 5)
                if has(i, 0):
                    after(pe, E["dots_ready"], i - 4)
                    if not has(i, -4):
                        after(pe, E["k_ready"], i + 1)
                    nc.tensor.matmul(ps_b[0:SK, 0:D], cT[:, r0, :], wvT, start=True, stop=True).then_inc(E["v_done"], 1)
                    after(pe, E["sub0"], i - 1)
                    scores(r0, 0).then_inc(E["s0_done"], 1)
                if has(i, 1):
                    after(pe, E["xn_ready"], i + 1)
                    after(pe, E["x2_ready"], i - 2)
                    if not has(i, -2):
                        after(pe, E["q_ready"], i)
                    nc.tensor.transpose(ps_a[:, 0:P], xn[:, r1, :], identf[:, :]).then_inc(E["xT_done"], 1)
                if has(i, 2):
                    after_dma(pe, c_loaded, i + 2, (m + 2) % RING)
                    after(pe, E["v_ready"], i)
                    if not has(i, 0):
                        after(pe, E["k_ready"], i + 1)
                    nc.tensor.transpose(ps_b[:, 0:SK], cin[0:SK, (m + 2) % RING, :], identf[0:SK, 0:SK]).then_inc(E["cT_done"], 1)
                if has(i, -1):
                    after(pe, E["exp_done"], i - 1)
                    probs_T(i - 1, r1, 0)
                    probs_T(i - 1, r1, 1)
                if has(i, 0):
                    after(pe, E["sub1"], i - 1)
                    scores(r0, 1, last=False)
                if has(i, -3):
                    turn(i, m)
                if has(i, 2):
                    after(pe, E["cT_ready"], i + 2)
                    nc.tensor.matmul(ps_b[:, 0:SK], wkT, cT[:, r0, :], start=True, stop=True).then_inc(E["k_done"], 1)
                if known(i) and i == NB - 1:
                    pe.wait_ge(skip_ready, 1)
                if has(i, -1):
                    after(pe, E["recx_ready"], i - 1)
                    after(pe, E["rk_ready"], i - 5)
                    nc.tensor.transpose(ps_o[:, P:2 * P], recx[:, r1, :], identf[:, :]).then_inc(E["recT_done"], 1)
                    after(pe, E["t0_ready"], i - 1)
                    probs_T(i - 1, r1, 2)
                    after(pe, E["t1_ready"], i - 1)
                    probs_T(i - 1, r1, 3)
                if has(i, 0):
                    scores(r0, 1, first=False).then_inc(E["s1_done"], 1)
                if has(i, 1):
                    if not has(i, -3):
                        after(pe, E["xT_ready"], i + 1)
                    after(pe, E["xn2T_ready"], i - 3)
                    nc.tensor.matmul(ps_a[:, 0:P], wqT, xT[:, r1, :], start=True, stop=True).then_inc(E["q_done"], 1)
                if has(i, -3):
                    gate(i, r1)
                if has(i, -4):
                    rank(i, r0)
                if has(i, -1):
                    after(pe, E["t3_ready"], i - 1)
                    if not has(i, 1):
                        after(pe, E["v_ready"], i - 1)
                    if not has(i, -4):
                        after(pe, E["recT_ready"], i - 1)
                    for j in range(HG):
                        for g in range(G):
                            last = nc.tensor.matmul(ps_o[g * QR:(g + 1) * QR, 0:P], vpad[0:SK, r1, g, j * QR:(j + 1) * QR],
                                                    pT[0:SK, g, j * P:(j + 1) * P], start=(j == 0), stop=(j == HG - 1),
                                                    tile_position=(0, g * QR))
                    last.then_inc(E["av_done"], 1)

            step(-2, -2)
            pe.wait_ge(sim_dir, 1)
            nc.tensor.transpose(ps_o[:, 0:NE], simd[:, :], identf[0:NE, 0:NE]).then_inc(simt_done, 1)
            step(-1, -1)
            pe.wait_ge(simt_copied, 1)
            nc.tensor.matmul(ps_o[:, 0:NE], wnat[:, 4, :], simT[:, :], start=True, stop=True).then_inc(wgp_done, 1)
            pe.wait_ge(mask_ready, 1)
            step(0, 0)
            pe.wait_ge(wgp_copied, 1)
            pe.wait_ge(wpt_copied, 2)
            steps(pe, step, 1, NB - 1, 5, PART)

            def count_rows():
                after(pe, E["selsum_ready"], NB - 1)
                after(pe, E["rk_ready"], NB - 1)
                nc.tensor.matmul(ps_b[:, 0:NE], onesb[:, :], selsum[:, NB % 2, :], start=True, stop=True).then_inc(cnt_done, 1)

            step(NB, NB)
            pe.wait_ge(tab_ready, 3)
            pe.wait_ge(l_ffn, 16 * 3)
            ps_x = [ps_t[:, 0, :], ps_t[:, 1, :]]

            def tile(j, m):
                if has(j, 2, N_TILES):
                    r, q = m % 2, (m + 2) % FRING
                    after_dma(pe, xt_loaded, j + 2, q)
                    after(pe, FE["xtT_ready"], j)
                    nc.tensor.transpose(ps_x[r][:, 0:P], xt[:, q, 0:D], identf[:, :]).then_inc(FE["xtT_done"], 1)
                if has(j, 1, N_TILES):
                    r = (m + 1) % 2
                    after(pe, FE["xtT_ready"], j + 1)
                    after(pe, FE["w1c_ready"], j + 1)
                    after(pe, FE["h_ready"], j - 1)
                    for c in range(FC):
                        last = nc.tensor.matmul(ps_s[:, r, c * P:(c + 1) * P], w1c[:, r, c * P:(c + 1) * P], xtT[:, r, :],
                                                start=True, stop=True)
                    last.then_inc(FE["up_done"], 1)
                if has(j, -1, N_TILES):
                    r = (m - 1) % 2
                    b = j - 1
                    e = pe.value_load(tab_w[0:1, b:b + 1] if known(b) else tab_w[0:1, bass.ds(b, 1)],
                                      min_val=0, max_val=(NE - 1) * F)
                    after(pe, FE["act_ready"], j - 1)
                    after(pe, FE["eo_ready"], b - 1 if m - 1 <= TWO_BANKS else b - 2)
                    for c in range(FC):
                        last = nc.tensor.matmul(down_bank(m - 1)[:, 0:D], hT[:, r, c * P:(c + 1) * P], w2s[:, bass.ds(e + c * D, D)],
                                                start=(c == 0), stop=(c == FC - 1))
                    last.then_inc(FE["down_done"], 1)

            def between(j):
                r = (NB + 1) % 2
                if j == 0:
                    project(NB + 1, r)
                elif j == 1:
                    turn(NB + 1, NB + 1)
                elif j == 2:
                    gate(NB + 1, 1 - r)
                elif j == 4:
                    turn(NB + 2, NB + 2)
                elif j == 6:
                    gate(NB + 2, r)
                elif j in (5, 11, 17):
                    rank(NB + 1 + j // 6, (NB + 1 + j // 6) % 2)
                elif j == DRAINED - 1:
                    count_rows()
                elif j == DRAINED + 8:
                    tables(1, NB - 1)
                elif j == DRAINED + 11:
                    pe.wait_ge(tab_ready, 5)

            steps(pe, tile, -2, N_TILES, DRAINED + 11, N_TILES - 3, FRING, between)

        @block.scalar
        def _(act):
            for n, w in ((2, w_v), (3, w_o), (4, w_p)):
                act.dma_start(wnat[:, n, :], w).then_inc(l_w, 16)
            act.dma_start(bk[:, :], b_k.rearrange("(p o) -> p o", o=1)).then_inc(l_bqk, 16)
            act.dma_start(bq[:, :], b_q.rearrange("(p o) -> p o", o=1)).then_inc(l_bqk, 16)
            act.wait_ge(consts, N_CONSTS)
            nc.scalar.activation(warm[:, :], neghalf[:, :], ACT.Exp)
            act.wait_ge(wt_done, 1)
            nc.scalar.activation(wT[:, :, :].rearrange("p n m -> p (n m)"), ps_t[:, 0, :], ACT.Copy).then_inc(wt_copied, 1)
            act.wait_ge(l_sim, 16 * 2)
            nc.scalar.activation(sim_sq[:, :], simn[:, :], ACT.Square, accum_out=sim_n2[:, 0:1]).then_inc(sim_sqd, 1)
            act.wait_ge(l_bqk, 16 * 2)

            def probs_out(i, g):
                after(act, E[f"t{g}_done"], i - 1)
                after(act, E["av_done"], i - 2)
                nc.scalar.activation(pT[0:SK, g, :], ps_t[0:SK, g % 2, :], ACT.Copy).then_inc(E[f"t{g}_ready"], 1)

            def turned(i, r1):
                after(act, E["xn2T_done"], i - 3)
                after(act, E["g_done"], i - 5)
                nc.scalar.activation(xn2T[:, r1, :], ps_a[:, 0:P], ACT.Copy).then_inc(E["xn2T_ready"], 1)

            def gated(i, r1):
                after(act, E["g_done"], i - 3)
                after(act, E["ginv_ready"], i - 5)
                after(act, E["sq_ready"], i - 4)
                nc.scalar.activation(sq_junk[:, :], ps_b[:, 0:D], ACT.Square, accum_out=n2[:, r1:r1 + 1]
                                     ).then_inc(E["sq_ready"], 1)
                after(act, E["gv_ready"], i - 5)
                nc.scalar.activation(dots[:, r1, :], ps_b[:, D:D + NE], ACT.Copy).then_inc(E["dots_ready"], 1)

            def step(i, m):
                r0, r1 = m % 2, (m + 1) % 2
                if has(i, 0):
                    after(act, E["t3_done"], i - 2)
                    after(act, E["rec_ready"], i - 2)
                    after(act, E["max2"], i)
                    for hd in range(2 * HB, H):
                        c = (hd - 2 * HB) * SK
                        last = nc.scalar.activation(pr[:, r0, hd, :], ps_s[:, 2, c:c + SK], ACT.Exp, bias=mx[:, r0, hd:hd + 1],
                                                    accum_out=sums[:, r0, hd:hd + 1])
                    last.then_inc(E["exp2_done"], 1)
                if has(i, 1):
                    after(act, E["xT_done"], i + 1)
                    after(act, E["q_done"], i - 1)
                    nc.scalar.activation(xT[:, r1, :], ps_a[:, 0:P], ACT.Copy).then_inc(E["xT_ready"], 1)
                if has(i, 2):
                    after(act, E["cT_done"], i + 2)
                    after(act, E["v_done"], i)
                    after(act, E["k_done"], i)
                    nc.scalar.activation(cT[:, r0, :], ps_b[:, 0:SK], ACT.Copy).then_inc(E["cT_ready"], 1)
                if has(i, -1):
                    probs_out(i, 0)
                    probs_out(i, 1)
                if has(i, -3):
                    turned(i, r1)
                if has(i, 2):
                    after(act, E["k_done"], i + 2)
                    after(act, E["kbd_ready"], i)
                    nc.scalar.activation(kT[:, r0, :], ps_b[:, 0:SK], ACT.Identity, bias=bk[:, 0:1]).then_inc(E["k_ready"], 1)
                if has(i, -1):
                    after(act, E["recT_done"], i - 1)
                    after(act, E["cx_ready"], i - 3)
                    nc.scalar.activation(recT[:, r1, :], ps_o[:, P:2 * P], ACT.Copy).then_inc(E["recT_ready"], 1)
                    probs_out(i, 2)
                    probs_out(i, 3)
                if has(i, 1):
                    after(act, E["q_done"], i + 1)
                    after(act, E["s1_done"], i - 1)
                    for g in range(G):
                        rws = slice(g * QR, (g + 1) * QR)
                        last = nc.scalar.activation(qz[rws, r1, g, :], ps_a[rws, 0:P], ACT.Identity, bias=bqs[rws, 0:1], scale=SCALE)
                    last.then_inc(E["q_ready"], 1)
                if has(i, -3):
                    gated(i, r1)
                if has(i, 0):
                    after(act, E["sub1"], i)
                    p = pr[:, r0, 0:2 * HB, :].rearrange("p h k -> p (h k)")
                    nc.scalar.activation(p, p, ACT.Exp).then_inc(E["exp_done"], 1)

            step(-2, -2)
            act.wait_ge(sim_inv, 2)
            nc.scalar.activation(simd[:, :], simn[:, :], ACT.Copy, scale=sim_n2[:, 2:3]).then_inc(sim_dir, 1)
            act.wait_ge(wt_done, 2)
            nc.scalar.activation(wg[:, 0:D], ps_t[:, 1, 0:P], ACT.Copy).then_inc(wpt_copied, 1)
            nc.scalar.activation(b1T[:, 0:NE * FC], ps_t[:, 1, P:P + NE * FC], ACT.Copy).then_inc(wpt_copied, 1)
            act.wait_ge(simt_done, 1)
            nc.scalar.activation(simT[:, :], ps_o[:, 0:NE], ACT.Copy).then_inc(simt_copied, 1)
            act.wait_ge(vzero, 4)
            act.wait_ge(bqs_ready, 1)
            step(-1, -1)
            act.wait_ge(wgp_done, 1)
            nc.scalar.activation(wg[:, D:D + NE], ps_o[:, 0:NE], ACT.Copy).then_inc(wgp_copied, 1)
            steps(act, step, 0, NB, 5, NB - 3)

            act.wait_ge(l_ffn, 16 * 3)
            act.wait_ge(tab_ready, 3)

            def tile(j, m):
                r = m % 2
                if has(j, 2, N_TILES):
                    b = j + 2
                    e = act.value_load(tab_w[0:1, b:b + 1] if known(b) else tab_w[0:1, bass.ds(b, 1)],
                                       min_val=0, max_val=(NE - 1) * F)
                    after(act, FE["up_done"], j)
                    settled(act)
                    nc.scalar.activation(w1c[:, r, :], w1s[:, bass.ds(e, F)], ACT.Copy).then_inc(FE["w1c_ready"], 1)
                if has(j, 0, N_TILES):
                    after(act, FE["h_ready"], j)
                    after(act, FE["down_done"], j - 2)
                    nc.scalar.activation(hT[:, r, :], h[:, r, :], ACT.Gelu).then_inc(FE["act_ready"], 1)

            def between(j):
                r = (NB + 1) % 2
                if j == 2:
                    turned(NB + 1, 1 - r)
                elif j == 3:
                    gated(NB + 1, 1 - r)
                elif j == 5:
                    turned(NB + 2, r)
                elif j == 7:
                    gated(NB + 2, r)
                elif j == DRAINED + 11:
                    act.wait_ge(tab_ready, 5)

            steps(act, tile, -2, N_TILES - 1, DRAINED + 11, N_TILES - 3, FRING, between)

            act.wait_ge(E["diff_ready"], NB)
            nc.scalar.activation(expd[:, :], diff[:, :], ACT.Exp).then_inc(p_step, 1)

            act.wait_ge(p_step, 5)
            for c in range(NB // CH):
                after_y(act, c)
                for b in range(c * CH, (c + 1) * CH):
                    if on_pool(b):
                        for k, p in enumerate((p1, p2)):
                            y = ys[:, c, k, b % CH, :]
                            nc.scalar.activation(y, y, ACT.Copy, scale=p[:, b:b + 1]).then_inc(weighted, 1)

        @block.vector
        def _(dve):
            nc.vector.memset(vpad[:, :, :, :], 0.0).then_inc(vzero, 1)
            nc.vector.memset(ones16[:, :], 1.0).then_inc(vzero, 1)
            nc.vector.memset(rows[:, :, :, :], 0.0).then_inc(vzero, 1)
            nc.vector.memset(qz[:, :, :, :], 0.0).then_inc(vzero, 1)
            dve.wait_ge(vzero, 4)
            dve.wait_ge(consts, N_CONSTS)
            nc.vector.tensor_reduce(headmask4[:, :], headmask[:, :].rearrange("p (g j) -> p j g", g=G), AX.X, ALU.add
                                    ).then_inc(headmask4_ready, 1)
            dve.wait_ge(l_bqk, 16 * 2)
            nc.vector.tensor_scalar(bqs[:, :], bq[:, :], SCALE, None, ALU.mult).then_inc(bqs_ready, 1)

            def bank(n, nh):
                return ps_s[:, n, 0:nh * SK].rearrange("p (h k) -> p h k", k=SK)

            hs = 2 * HB

            def maximum(i, r, n, hd, nh):
                after(dve, E[f"s{n}_done"], i)
                nc.vector.tensor_reduce(mx[:, r, hd:hd + nh], bank(n, nh), AX.X, ALU.max, negate=True).then_inc(E[f"max{n}"], 1)

            def less_maximum(i, r, n):
                after(dve, E[f"max{n}"], i)
                after(dve, E["t3_done"], i - 2)
                hd = n * HB
                nc.vector.tensor_tensor(pr[:, r, hd:hd + HB, :], bank(n, HB), mx[:, r, hd:hd + HB].unsqueeze(2).to_broadcast([P, HB, SK]),
                                        ALU.add).then_inc(E[f"sub{n}"], 1)

            def rows_of_lists(i, r1):
                after(dve, E["rk_ready"], i - 5)
                nc.vector.tensor_tensor(prod[:, :, :], ohs[:, r1, :, :], rk[:, :].unsqueeze(1).to_broadcast([P, TOPK, NE]),
                                        ALU.mult).then_inc(E["prod_ready"], 1)

            def residual(i):
                after(dve, E["o_done"], i - 2)
                after(dve, E["xb_ready"], i - 2)
                nc.vector.tensor_tensor(at(x2, i - 2), ps_a[:, 0:D], at(x2, i - 2), ALU.add).then_inc(E["x2_ready"], 1)

            def rows_taken(i, m):
                b, r = i - 5, (m - 5) % RING
                after(dve, E["prod_ready"], b)
                with nc.allow_low_precision(reason="rows are whole numbers below 2**24, summed in float32"):
                    nc.vector.tensor_reduce(slots[:, r, :], prod[:, :, :], AX.X, ALU.add).then_inc(E["slot_ready"], 1)

            def second_stats(i, r0):
                after(dve, E["x2_ready"], i - 2)
                settled(dve)
                nc.vector.bn_stats(st2[:, r0, :], at(x2, i - 2)).then_inc(E["bn2"], 1)

            def second_mean(i, r0):
                after(dve, E["bn2"], i - 2)
                settled(dve)
                nc.vector.bn_aggr(mv2[:, r0, :], st2[:, r0, :]).then_inc(E["ln2"], 1)

            def gates(i, r0):
                after(dve, E["ginv_ready"], i - 4)
                after(dve, E["dots_ready"], i - 4)
                nc.vector.tensor_scalar(gv[:, :], dots[:, r0, :], ginv[:, r0:r0 + 1], MASKED, ALU.mult, ALU.max
                                        ).then_inc(E["gv_ready"], 1)

            def best(i):
                after(dve, E["gv_ready"], i - 4)
                settled(dve)
                nc.vector.max(top8[:, :], gv[:, :]).then_inc(E["top_ready"], 1)

            def best_places(i):
                after(dve, E["top_ready"], i - 4)
                settled(dve)
                nc.vector.max_index(idx8[:, :], top8[:, :], gv[:, :]).then_inc(E["idx_ready"], 1)
                b = i - 4
                dcol = diff[:, b:b + 1] if known(b) else diff[:, bass.ds(b, 1)]
                nc.vector.tensor_tensor(dcol, top8[:, 1:2], top8[:, 0:1], ALU.subtract).then_inc(E["diff_ready"], 1)

            def one_hots(i, r0):
                after(dve, E["idx_ready"], i - 4)
                nc.vector.tensor_tensor(ohs[:, r0, :, :], iota_e[:, 0:NE].unsqueeze(1).to_broadcast([P, TOPK, NE]),
                                        idx8[:, 0:TOPK].unsqueeze(2).to_broadcast([P, TOPK, NE]), ALU.is_equal
                                        ).then_inc(E["ohs_ready"], 1)

            def chosen(i, r0):
                after(dve, E["ohs_ready"], i - 4)
                after(dve, E["rank_done"], i - 6)
                nc.vector.tensor_tensor(sel[:, r0, :], ohs[:, r0, 0, :], ohs[:, r0, 1, :], ALU.add).then_inc(E["sel_ready"], 1)

            def chosen_sum(i, r0, r1):
                after(dve, E["sel_ready"], i - 4)
                after(dve, E["rank_done"], i - 5)
                after(dve, E["selsum_ready"], i - 5)
                nc.vector.tensor_tensor(selsum[:, r1, :], selsum[:, r0, :], sel[:, r0, :], ALU.add
                                        ).then_inc(E["selsum_ready"], 1)

            def second_norm(i, m, r0):
                b, r = i - 2, (m - 2) % RING
                after(dve, E["rs2"], b)
                after(dve, E["xn2T_done"], b - RING)
                after_dma(dve, scattered, b - RING, r, 16 * TOPK)
                nc.vector.tensor_scalar(rows[:, r, :, 0:D], at(x2, b).unsqueeze(1).to_broadcast([P, TOPK, D]),
                                        mv2[:, r0, 0:1], rstd2[:, r0:r0 + 1], ALU.subtract, ALU.mult
                                        ).then_inc(E["xn2_ready"], 1)

            def ranks(i):
                after(dve, E["rank_done"], i - 4)
                if known(i) and i - 4 == PART:
                    nc.vector.tensor_copy(cnt0[:, :], ps_o[:, 272:272 + NE]).then_inc(cnt_done, 1)
                nc.vector.tensor_tensor(rk[:, :], ps_o[:, 256:256 + NE], list_base[:, 0, :], ALU.add).then_inc(E["rk_ready"], 1)

            tab_steps = [0]

            def written(*ins):
                for one in ins:
                    one.then_inc(tab_step, 1)
                tab_steps[0] += len(ins)

            def tables(part, stage):
                if stage == 0:
                    dve.wait_ge(cnt_done, part + 1)
                else:
                    dve.wait_ge(tab_step, tab_steps[0])
                W = NE * (part + 1)

                def twice(ap):
                    return ap.rearrange("p a e -> p (a e)")[:, 0:W]

                now = tiles0[:, 0, :] if part == 0 else upto[:, :]
                if part == 0 and stage == 0:
                    written(nc.vector.tensor_copy(tiles_i[:, 0, 0, :], cnt0[:, :]),
                            nc.vector.tensor_scalar(tiles_i[:, 0, 1, :], cnt0[:, :], float(P - 1), None, ALU.add),
                            nc.vector.scalar_tensor_tensor(starts[:, 1, 0, :], cnt0[:, :], -float(P), list_base[:, 0, :],
                                                           ALU.add, ALU.add))
                elif part == 0 and stage == 1:
                    written(nc.vector.tensor_scalar(tiles_i[:, 1, :, :], tiles_i[:, 0, :, :], P.bit_length() - 1, None,
                                                    ALU.arith_shift_right))
                elif part == 0 and stage == 2:
                    written(nc.vector.tensor_copy(tiles0[:, :, :], tiles_i[:, 1, :, :]))
                elif part == 0 and stage == 3:
                    written(nc.vector.tensor_tensor_scan(cum[:, 0:W], ones16[:, 0:W], now, 0.0, ALU.mult, ALU.add))
                elif part == 1 and stage == 0:
                    written(nc.vector.tensor_copy(cnt[:, :], ps_b[:, 0:NE]))
                elif part == 1 and stage == 1:
                    written(nc.vector.tensor_scalar(tiles_i[:, 0, 0, :], cnt[:, :], float(P - 1), None, ALU.add),
                            nc.vector.scalar_tensor_tensor(starts[:, 1, :, :], cnt[:, :].unsqueeze(1).to_broadcast([P, 2, NE]),
                                                           -float(P), list_base[:, :, :], ALU.add, ALU.add))
                elif part == 1 and stage == 2:
                    written(nc.vector.tensor_scalar(tiles_i[:, 1, 0, :], tiles_i[:, 0, 0, :], P.bit_length() - 1, None,
                                                    ALU.arith_shift_right))
                elif part == 1 and stage == 3:
                    written(nc.vector.tensor_copy(tiles1[:, :], tiles_i[:, 1, 0, :]))
                elif part == 1 and stage == 4:
                    written(nc.vector.tensor_tensor(todo[:, 0:NE], tiles0[:, 1, :], done[:, 0:NE], ALU.subtract),
                            nc.vector.tensor_tensor(todo[:, NE:W], tiles1[:, :], tiles0[:, 1, :], ALU.subtract),
                            nc.vector.tensor_copy(done[:, NE:W], tiles0[:, 1, :]))
                elif part == 1 and stage == 5:
                    written(nc.vector.tensor_tensor_scan(cum[:, :], ones16[:, :], todo[:, :], 0.0, ALU.mult, ALU.add),
                            nc.vector.tensor_tensor(upto[:, :], done[:, :], todo[:, :], ALU.add))
                elif stage == HEADS[part]:
                    written(nc.vector.tensor_tensor(ahead[:, 0:W], now, cum[:, 0:W], ALU.subtract),
                            nc.vector.tensor_scalar(cmp[:, 0:W], cum[:, 0:W], iota_p[:, 0:1], None, ALU.is_le))
                elif stage == HEADS[part] + 1:
                    written(nc.vector.scalar_tensor_tensor(twice(starts[:, 0, :, :]), ahead[:, 0:W], float(P),
                                                           twice(list_base[:, :, :]), ALU.mult, ALU.add),
                            nc.vector.tensor_reduce(which[:, :], cmp[:, 0:W], AX.X, ALU.add))
                    if part == 0:
                        written(nc.vector.tensor_scalar(upto[:, 0:NE], ahead[:, 0:NE], float(FULL_TILES), 0.0, ALU.add, ALU.max))
                elif stage == HEADS[part] + 2:
                    written(nc.vector.tensor_scalar(oh_t[:, 0:W], iota_e[:, 0:W], which[:, 0:1], None, ALU.is_equal))
                    if part == 0:
                        written(nc.vector.tensor_tensor(done[:, 0:NE], upto[:, 0:NE], tiles0[:, 0, :], ALU.min))
                elif stage == HEADS[part] + 3:
                    written(nc.vector.tensor_tensor(start_oh[:, :, 0:W], starts[:, :, :, :].rearrange("p n a e -> p n (a e)")[:, :, 0:W],
                                                    oh_t[:, 0:W].unsqueeze(1).to_broadcast([P, 3, W]), ALU.mult))
                elif stage == HEADS[part] + 4:
                    written(nc.vector.tensor_reduce(start[:, :], start_oh[:, :, 0:W], AX.X, ALU.add))
                elif stage == HEADS[part] + 5:
                    written(nc.vector.scalar_tensor_tensor(first[:, :], iota_p[:, :], float(P), start[:, 0:1], ALU.mult, ALU.add))
                elif stage == HEADS[part] + 6:
                    nc.vector.tensor_copy(cols[:, 0:1], start[:, 2:3]).then_inc(cols_ready, 1)
                    nc.vector.tensor_tensor(cols[:, 1:2], first[:, :], start[:, 1:2], ALU.min).then_inc(cols_ready, 1)
                elif stage == HEADS[part] + 7:
                    dve.wait_ge(cols_ready, 2 * (part + 1))
                    nc.vector.tensor_tensor(again[:, :], first[:, 0:1].to_broadcast([P, P]), cols[:, 1:2].to_broadcast([P, P]),
                                            ALU.subtract).then_inc(again_ready, 1)

            def table_rows(part):
                a = 0 if part == 0 else PART_TILES[0]
                z = PART_TILES[0] if part == 0 else TT
                dve.wait_ge(again_T, part + 1)
                nc.vector.tensor_scalar(bias_at[:, a:z], tabs[0][0:1, 0:z - a], float(FC) / F, None, ALU.mult
                                        ).then_inc(bias_step, 1)
                nc.vector.tensor_copy(tab_w[:, a:z], tabs[0][0:1, 0:z - a]).then_inc(tab_ready, 1)
                nc.vector.tensor_copy(tab_r[:, a:z], tabs[1][0:1, 0:z - a]).then_inc(rows_ready, 1)
                nc.vector.tensor_scalar(skip[:, a:z], tabs[2][:, 0:z - a], iota_p[:, 0:1], float(SKIP), ALU.is_gt, ALU.mult
                                        ).then_inc(skip_ready, 1)
                dve.wait_ge(bias_step, part + 1)
                if part == 0:
                    nc.vector.tensor_copy(tab_b[:, 0:AHEAD], bias_at[:, 0:AHEAD]).then_inc(tab_ready, 1)
                    a = AHEAD
                nc.vector.scalar_tensor_tensor(tab_b[:, a:z], bias_at[:, a - AHEAD:z - AHEAD], 32.0, bias_at[:, a:z],
                                               ALU.mult, ALU.add).then_inc(tab_ready, 1)

            def some_tables(i, n):
                stage = (i - PART - 5) * 8 + n if known(i) else -1
                if 0 <= stage < TAB_STAGES[0]:
                    tables(0, stage)

            def step(i, m):
                r0, r1 = m % 2, (m + 1) % 2
                if has(i, -5):
                    rows_of_lists(i, r1)
                some_tables(i, 0)
                if has(i, 0):
                    maximum(i, r0, 2, hs, H - hs)
                if has(i, -2):
                    residual(i)
                if known(i) and i == NB - 1:
                    table_rows(0)
                some_tables(i, 1)
                if has(i, 0):
                    after(dve, E["v_done"], i)
                    after(dve, E["av_done"], i - 2)
                    nc.vector.tensor_tensor(
                        vpad[0:SK, r0, :, :].rearrange("p g (j c) -> p g j c", j=HG)[:, :, :, 0:DH],
                        ps_b[0:SK, 0:D].rearrange("p (g j c) -> p g j c", g=G, j=HG),
                        bv[0:SK, :].rearrange("p (g j c) -> p g j c", g=G, j=HG), ALU.add).then_inc(E["v_ready"], 1)
                if has(i, -5):
                    rows_taken(i, m)
                some_tables(i, 2)
                if has(i, -2):
                    second_stats(i, r0)
                if has(i, -1):
                    after(dve, E["exp_done"], i - 1)
                    nc.vector.tensor_reduce(sums[:, r1, 0:hs], pr[:, r1, 0:hs, :], AX.X, ALU.add).then_inc(E["sums_ready"], 1)
                if has(i, -2):
                    second_mean(i, r0)
                some_tables(i, 3)
                if has(i, -4):
                    gates(i, r0)
                if has(i, -1):
                    after(dve, E["exp2_done"], i - 1)
                    after(dve, E["sums_ready"], i - 1)
                    nc.vector.reciprocal(rec[:, r1, :], sums[:, r1, :]).then_inc(E["rec_ready"], 1)
                some_tables(i, 4)
                if has(i, 3):
                    b, r = i + 3, (m + 3) % RING
                    after_dma(dve, x_loaded, b, r)
                    settled(dve)
                    nc.vector.bn_stats(st1[:, r, :], xin[:, r, :]).then_inc(E["bn1"], 1)
                if has(i, -4):
                    best(i)
                if has(i, -1):
                    after(dve, E["rec_ready"], i - 1)
                    after(dve, E["recT_done"], i - 3)
                    nc.vector.tensor_copy(recx[:, r1, :].rearrange("p (h d) -> p h d", d=DH),
                                          rec[:, r1, :].unsqueeze(2).to_broadcast([P, H, DH])).then_inc(E["recx_ready"], 1)
                if has(i, 3):
                    after(dve, E["bn1"], i + 3)
                    settled(dve)
                    nc.vector.bn_aggr(mv1[:, r, :], st1[:, r, :]).then_inc(E["ln1"], 1)
                if has(i, -4):
                    best_places(i)
                if has(i, 0):
                    maximum(i, r0, 0, 0, HB)
                if has(i, -4):
                    one_hots(i, r0)
                some_tables(i, 5)
                if has(i, 2):
                    r = (m + 2) % RING
                    after(dve, E["rs1"], i + 2)
                    after(dve, E["xT_done"], i)
                    nc.vector.tensor_scalar(xn[:, r0, :], xin[:, r, :], mv1[:, r, 0:1], rstd1[:, r:r + 1],
                                            ALU.subtract, ALU.mult).then_inc(E["xn_ready"], 1)
                if has(i, -4):
                    chosen(i, r0)
                some_tables(i, 6)
                if has(i, 0):
                    less_maximum(i, r0, 0)
                    maximum(i, r0, 1, HB, HB)
                if has(i, 0):
                    less_maximum(i, r0, 1)
                if has(i, -4):
                    chosen_sum(i, r0, r1)
                some_tables(i, 7)
                if has(i, -2):
                    second_norm(i, m, r0)
                if has(i, -1):
                    after(dve, E["recT_ready"], i - 1)
                    after(dve, E["o_done"], i - 3)
                    after(dve, E["av_done"], i - 1)
                    nc.vector.tensor_tensor(cxT[:, r1, :], ps_o[:, 0:P], recT[:, r1, :], ALU.mult).then_inc(E["cx_ready"], 1)
                if has(i, -4) and not (known(i) and i > NB):
                    ranks(i)

            step(-3, -3)
            step(-2, -2)
            dve.wait_ge(l_mask, 16)
            nc.vector.tensor_scalar(negb[:, :, :], maski[:, :].unsqueeze(1).to_broadcast([P, HB, SK]), 0.0, MASKED,
                                    ALU.is_equal, ALU.mult).then_inc(mask_ready, 1)
            nc.vector.tensor_scalar(maskn[:, :], maski[:, :], 0.0, None, ALU.not_equal).then_inc(mask_step, 1)
            dve.wait_ge(mask_step, 1)
            nc.vector.tensor_reduce(anyk[:, 0:1], maskn[:, :], AX.X, ALU.max).then_inc(mask_step, 1)
            dve.wait_ge(mask_step, 2)
            nc.vector.reciprocal(anyk[:, 1:2], anyk[:, 0:1]).then_inc(mask_step, 1)
            dve.wait_ge(mask_step, 3)
            nc.vector.tensor_scalar(anyk[:, 2:3], anyk[:, 1:2], 0.0, None, ALU.mult).then_inc(mask_step, 1)
            dve.wait_ge(mask_step, 4)
            dve.wait_ge(l_rows, 16 * 3)
            nc.vector.reciprocal(invtemp[:, :], tempc[:, :]).then_inc(itemp, 1)
            nc.vector.tensor_scalar(bo[:, :], bo_row[:, :], anyk[:, 2:3], None, ALU.add).then_inc(bo_ready, 1)
            steps(dve, step, -1, NB, 6, NB - 4)

            dve.wait_ge(tab_ready, 3)
            dve.wait_ge(wpt_copied, 2)
            dve.wait_ge(l_ffn, 16 * 3)
            ps_x = [ps_t[:, 0, :], ps_t[:, 1, :]]

            def tile(j, m):
                t = j - 1 + AHEAD
                if has(j, -1, N_TILES) or has(t, 0, N_TILES):
                    both = dve.value_load(tab_b[0:1, t:t + 1] if known(t) else tab_b[0:1, bass.ds(t, 1)],
                                          min_val=0, max_val=33 * (NE - 1) * FC)
                    e1, e2 = both % 32, both // 32 * (D // FC)
                if has(j, -1, N_TILES):
                    q = (m - 1) % FRING
                    after_dma(dve, returned, j - 1 - FRING, q)
                    after(dve, FE["down_done"], j - 1)
                    nc.vector.tensor_tensor(eo[:, q, :], down_bank(m - 1)[:, 0:D], b2s[:, bass.ds(e2, D)], ALU.add
                                            ).then_inc(FE["eo_ready"], 1)
                if has(j, 3, N_TILES):
                    r = (m + 1) % 2
                    after(dve, FE["up_done"], j + 1)
                    after(dve, FE["xtT_done"], j + 3)
                    nc.vector.tensor_copy(xtT[:, r, :], ps_x[r][:, 0:P]).then_inc(FE["xtT_ready"], 1)
                if has(j, 2, N_TILES):
                    r = m % 2
                    after(dve, FE["act_ready"], j)
                    after(dve, FE["up_done"], j + 2)
                    nc.vector.tensor_tensor(h[:, r, :].rearrange("p (c t) -> p c t", c=FC),
                                            ps_s[:, r, :].rearrange("p (c t) -> p c t", c=FC),
                                            b1T[:, bass.ds(e1, FC)].unsqueeze(2).to_broadcast([P, FC, P]), ALU.add
                                            ).then_inc(FE["h_ready"], 1)

            def between(j):
                r = (NB + 1) % 2
                if j == -1:
                    rows_of_lists(NB + 1, 1 - r)
                    residual(NB + 1)
                    rows_taken(NB + 1, NB + 1)
                    second_stats(NB + 1, r)
                    second_mean(NB + 1, r)
                elif j == 0:
                    second_norm(NB + 1, NB + 1, r)
                elif 0 < j < DRAINED - 1:
                    i = NB + 1 + (j - 1) // 6
                    r0, r1 = i % 2, (i + 1) % 2
                    if j % 6 == 1:
                        gates(i, r0)
                        best(i)
                    elif j % 6 == 2:
                        best_places(i)
                        one_hots(i, r0)
                    elif j % 6 == 3:
                        chosen(i, r0)
                        chosen_sum(i, r0, r1)
                    elif j % 6 == 5:
                        ranks(i)
                    elif j % 6 == 0:
                        rows_of_lists(i + 1, r0)
                        rows_taken(i + 1, i + 1)
                elif DRAINED <= j < DRAINED + 7:
                    for stage in range((j - DRAINED) * 2, (j - DRAINED) * 2 + 2):
                        tables(1, stage)
                elif j == DRAINED + 8:
                    table_rows(1)
                elif j == DRAINED + 11:
                    dve.wait_ge(tab_ready, 5)

            steps(dve, tile, -3, N_TILES, DRAINED + 11, N_TILES - 4, FRING, between)

            nc.vector.memset(den[:, :], 1.0).then_inc(p_step, 1)
            dve.wait_ge(p_step, 2)
            nc.vector.tensor_tensor(den[:, :], den[:, :], expd[:, :], ALU.add).then_inc(p_step, 1)
            dve.wait_ge(p_step, 3)
            nc.vector.reciprocal(p1[:, :], den[:, :]).then_inc(p_step, 1)
            dve.wait_ge(p_step, 4)
            nc.vector.tensor_tensor(p2[:, :], expd[:, :], p1[:, :], ALU.mult).then_inc(p_step, 1)

            dve.wait_ge(p_step, 5)
            for c in range(NB // CH):
                mine = [b for b in range(c * CH, (c + 1) * CH) if not on_pool(b)]
                after_y(dve, c)
                for b in mine:
                    nc.vector.scalar_tensor_tensor(x2[:, b, :], ys[:, c, 0, b % CH, :], p1[:, b:b + 1], x2[:, b, :],
                                                   ALU.mult, ALU.add).then_inc(sum1, 1)
                for b in mine:
                    dve.wait_ge(sum1, summed_before(b + 1, False))
                    nc.vector.scalar_tensor_tensor(x2[:, b, :], ys[:, c, 1, b % CH, :], p2[:, b:b + 1], x2[:, b, :],
                                                   ALU.mult, ALU.add).then_inc(sum2, 1)


_INS = ['x', 'ctx_1024', 'mask_1x1xSxS2_ik0', 'L0_xattn_W_q', 'L0_xattn_b_q', 'L0_xattn_W_k', 'L0_xattn_b_k',
        'L0_xattn_W_v', 'L0_xattn_b_v', 'L0_xattn_W_o', 'L0_xattn_b_o', 'L0_ffn_Wp', 'L0_ffn_sim_matrix',
        'L0_ffn_temperature', 'L0_ffn_W1', 'L0_ffn_b1', 'L0_ffn_W2', 'L0_ffn_b2']
_OUTS = [((32, 128, 128), 'float32')]


def kernel(**inputs):
    import numpy as _np
    import concourse.bacc as _bacc
    from concourse import mybir as _mybir
    from concourse.bass_utils import run_bass_kernel_spmd as _run

    nc = _bacc.Bacc("TRN2", target_bir_lowering=False, num_devices=1)
    arrays, args = {}, []
    for name in _INS:
        a = _np.ascontiguousarray(inputs[name])
        arrays[f"in_{name}_dram"] = a
        args.append(nc.dram_tensor(f"in_{name}_dram", a.shape, _mybir.dt.from_np(a.dtype), kind="ExternalInput").ap())
    for i, (shape, dtype) in enumerate(_OUTS):
        dt = _mybir.dt.from_np(_np.dtype(dtype))
        args.append(nc.dram_tensor(f"out_{i}_dram", shape, dt, kind="ExternalOutput").ap())
    xattn_moe_kernel(nc, *args)
    r = _run(nc, [arrays], core_ids=[0])
    got = tuple(r.results[0][f"out_{i}_dram"] for i in range(len(_OUTS)))
    return got[0]
```
